# Optimizing a Trainium2 kernel written in Bass

```python
import numpy as np
import jax
import jax.numpy as jnp

def _softmax(x, axis=-1):
    return jax.nn.softmax(x, axis=axis)

def _gelu(x):
    return jax.nn.gelu(x, approximate=True)

def _silu(x):
    return jax.nn.silu(x)

def _sigmoid(x):
    return jax.nn.sigmoid(x)

def _layernorm(x, axis=-1, eps=1e-05):
    m = jnp.mean(x, axis=axis, keepdims=True)
    v = jnp.var(x, axis=axis, keepdims=True)
    return (x - m) / jnp.sqrt(v + eps)

def _scatter_add(tgt, idx, src, axis=0):
    return tgt.at[idx].add(src)

def _segment_sum(src, seg, n):
    return jax.ops.segment_sum(src, seg, n)
kernel_name = 'mk_seq_preln_d1_jaxref_r4_1837bf'

def setup_inputs(seed: int=0):
    np.random.seed(seed)
    _w = jnp.asarray

    def _L0_attn_setup():
        import jax, jax.numpy as jnp
        import numpy as np
        MAX_WAVELENGTH = 10000.0
        NEG_INF = -1000000000.0

        def apply_rope(x):
            S, D = (x.shape[1], x.shape[-1])
            inv_freq = 1.0 / MAX_WAVELENGTH ** (jnp.arange(0, D, 2, dtype=jnp.float32) / D)
            t = jnp.arange(S, dtype=jnp.float32)[:, None] * inv_freq[None, :]
            emb = jnp.concatenate([t, t], axis=-1)
            cos = jnp.cos(emb)[None, :, None, :].astype(x.dtype)
            sin = jnp.sin(emb)[None, :, None, :].astype(x.dtype)
            x1, x2 = jnp.split(x, 2, axis=-1)
            rotated = jnp.concatenate([-x2, x1], axis=-1)
            return x * cos + rotated * sin
        key = jax.random.key(seed)
        k1, k2, k3 = jax.random.split(key, 3)
        B, S, dim = (2, 512, 256)
        x = jax.random.normal(k1, (B, S, dim), dtype=jnp.float32)
        w_qkv = jax.random.normal(k2, (dim, 3 * dim), dtype=jnp.float32) * dim ** (-0.5)
        w_proj = jax.random.normal(k3, (dim, dim), dtype=jnp.float32) * dim ** (-0.5)
        b_proj = jnp.zeros((dim,), dtype=jnp.float32)
        return {'x': x, 'w_qkv': w_qkv, 'w_proj': w_proj, 'b_proj': b_proj}
    _L0_attn_in = _L0_attn_setup()

    def _L0_ffn_setup():
        import jax, jax.numpy as jnp
        import numpy as np
        INPUT_SIZE = 256
        OUTPUT_SIZE = 256
        key = jax.random.key(seed)
        kx, kt, kp, ktn, kpn = jax.random.split(key, 5)
        x = jax.random.normal(kx, (8, 512, INPUT_SIZE), dtype=jnp.float32)
        theta = jax.random.normal(kt, (INPUT_SIZE, OUTPUT_SIZE), dtype=jnp.float32) * 0.02
        phi = jax.random.normal(kp, (INPUT_SIZE, OUTPUT_SIZE), dtype=jnp.float32) * 0.02
        theta_noise = jax.random.normal(ktn, (INPUT_SIZE, OUTPUT_SIZE), dtype=jnp.float32) * 0.01
        phi_noise = jax.random.normal(kpn, (INPUT_SIZE, OUTPUT_SIZE), dtype=jnp.float32) * 0.01
        return {'x': x, 'theta': theta, 'phi': phi, 'theta_noise': theta_noise, 'phi_noise': phi_noise}
    _L0_ffn_in = _L0_ffn_setup()
    _d = {'L0_attn_x': _L0_attn_in['x'], 'L0_attn_w_qkv': _L0_attn_in['w_qkv'], 'L0_attn_w_proj': _L0_attn_in['w_proj'], 'L0_attn_b_proj': _L0_attn_in['b_proj'], 'L0_ffn_theta': _L0_ffn_in['theta'], 'L0_ffn_phi': _L0_ffn_in['phi'], 'L0_ffn_theta_noise': _L0_ffn_in['theta_noise'], 'L0_ffn_phi_noise': _L0_ffn_in['phi_noise']}
    _x0 = _d['L0_attn_x']
    _d['L0_attn_x'] = jax.random.normal(jax.random.fold_in(jax.random.key(seed), 1), (4, 2048, 256), dtype=_x0.dtype)
    del _x0
    return _d

def reference(L0_attn_x, L0_attn_w_qkv, L0_attn_w_proj, L0_attn_b_proj, L0_ffn_theta, L0_ffn_phi, L0_ffn_theta_noise, L0_ffn_phi_noise):

    def _L0_attn_ref(x, w_qkv, w_proj, b_proj):
        import jax, jax.numpy as jnp
        import numpy as np
        MAX_WAVELENGTH = 10000.0
        NEG_INF = -1000000000.0

        def apply_rope(x):
            S, D = (x.shape[1], x.shape[-1])
            inv_freq = 1.0 / MAX_WAVELENGTH ** (jnp.arange(0, D, 2, dtype=jnp.float32) / D)
            t = jnp.arange(S, dtype=jnp.float32)[:, None] * inv_freq[None, :]
            emb = jnp.concatenate([t, t], axis=-1)
            cos = jnp.cos(emb)[None, :, None, :].astype(x.dtype)
            sin = jnp.sin(emb)[None, :, None, :].astype(x.dtype)
            x1, x2 = jnp.split(x, 2, axis=-1)
            rotated = jnp.concatenate([-x2, x1], axis=-1)
            return x * cos + rotated * sin
        B, S, dim = x.shape
        heads = 16
        head_dim = dim // heads
        scale = head_dim ** (-0.5)
        qkv = x @ w_qkv
        qkv = qkv.reshape(B, S, 3, heads, head_dim)
        Q, K, V = (qkv[:, :, 0], qkv[:, :, 1], qkv[:, :, 2])
        Q = apply_rope(Q)
        K = apply_rope(K)
        attn = jnp.einsum('bqhd,bkhd->bhqk', Q, K) * scale
        causal = jnp.tril(jnp.ones((S, S), dtype=bool))[None, None]
        attn = jnp.where(causal, attn, jnp.asarray(NEG_INF, attn.dtype))
        attn = jax.nn.softmax(attn, axis=-1)
        out = jnp.einsum('bhqk,bkhd->bqhd', attn, V).reshape(B, S, dim)
        return out @ w_proj + b_proj

    def _L0_ffn_ref(x, theta, phi, theta_noise, phi_noise):
        import jax, jax.numpy as jnp
        import numpy as np
        INPUT_SIZE = 256
        OUTPUT_SIZE = 256
        real = jnp.einsum('bti,io->bto', x, jnp.cos(theta + theta_noise))
        imag = jnp.einsum('bti,io->bto', x, jnp.sin(phi + phi_noise))
        return jnp.sqrt(real * real + imag * imag)
    x = L0_attn_x
    x = x + _L0_attn_ref(_layernorm(x, axis=-1), L0_attn_w_qkv, L0_attn_w_proj, L0_attn_b_proj)
    x = x + _L0_ffn_ref(_layernorm(x, axis=-1), L0_ffn_theta, L0_ffn_phi, L0_ffn_theta_noise, L0_ffn_phi_noise)
    return x

_drawn_inputs = setup_inputs


def setup_inputs(seed=0):
    import zlib

    import numpy as np

    out = dict(_drawn_inputs(seed))
    spreads = {'L0_attn_b_proj': (0.0, 0.1)}
    factors = {'L0_ffn_theta': 8.0, 'L0_ffn_theta_noise': 8.0}
    for name, (base, spread) in spreads.items():
        noise = np.random.default_rng([zlib.crc32(name.encode()), seed]).standard_normal(out[name].shape)
        drawn = base * np.exp(spread * noise) if base else spread * noise
        out[name] = jnp.asarray(drawn.astype(out[name].dtype))
    for name, factor in factors.items():
        out[name] = (out[name] * factor).astype(out[name].dtype)
    return out
```

```python
from contextlib import ExitStack

import numpy as np

import concourse.bass as bass
from concourse import mybir
from concourse.alu_op_type import AluOpType as ALU

ACT = mybir.ActivationFunctionType
AX = mybir.AxisListType
F32 = mybir.dt.float32
BF16 = mybir.dt.bfloat16

P = 128
BATCH, SEQ, DIM, HEADS = 4, 2048, 256, 16
HD = DIM // HEADS
HG = 4
GROUPS = HEADS // HG
UNITS = BATCH * GROUPS
KT = DIM // P
SPAN = 512
SPANS = SEQ // SPAN
SUB = SPAN // P
TILES = SEQ // P
BLOCKS = BATCH * SPANS
GF = HG * HD
VW = 32
EPS = 1e-5

PARTS = 6
SPLIT_ROWS = PARTS * HD
Q_SLOTS = [(0, 3, 1), (3, 6, 2), (4, 5, 1)]
K_SLOTS = [(2, 5, 1), (1, 6, 4), (0, 1, 1)]
MAX_ROWS = P - SPLIT_ROWS
NEG = -1e30

ROPE_OPS = 12
REDUCE_OPS = 10


def preparation():
    items = []

    def project(c):
        return [("qkv", c, 0), ("qkv", c, 1)]

    def rope(c):
        return [("rope", c, n) for n in range(ROPE_OPS)]

    def trans(c):
        return [("trans", SUB * c + j) for j in range(SUB)]

    def maxima(t):
        return [("max", SUB * t + j, h, c) for j in range(SUB) for h in range(HG) for c in range(t + 1)]

    def mix(long, short):
        out, done = [], 0
        for n, x in enumerate(long):
            out.append(x)
            while done < len(short) and done * len(long) < (n + 1) * len(short):
                out.append(short[done])
                done += 1
        return out + short[done:]

    items += project(0)
    for i in rope(0):
        items += [i, None]
    items += trans(0) + project(1)
    for t in range(SPANS):
        tail = [("maxrows", t - 1, 0), ("maxrows", t - 1, 1)] if t else []
        chunks = maxima(t)
        head, rest = chunks[:4], chunks[4:]
        items += head + tail
        if t + 1 < SPANS:
            more = rope(t + 1) + trans(t + 1)
            if t + 2 < SPANS:
                more += project(t + 2)
            items += mix(rest, more) if len(rest) >= len(more) else mix(more, rest)
        else:
            items += rest
    items += [None] * 4 + [("maxrows", SPANS - 1, 0), ("maxrows", SPANS - 1, 1)]
    return items


ITEMS = preparation()
WEIGHT = {"qkv": 3.0, "rope": 0.1, "trans": 2.0, "max": 1.0, "maxrows": 1.0}
STEPS = [(t, j) for t in range(SPANS) for j in range(SUB * (t + 1))]
NSTEP = len(STEPS)
DIAG = SUB * SPANS
PLACES = 3


def widths(step):
    t, j = STEPS[step]
    return max(0, P * (j - SUB * t))


def spread():
    room = []
    for s in range(NSTEP):
        w = SPAN - widths(s)
        room += [w / 3 + 40] * PLACES
    total = sum(WEIGHT[i[0]] if i else 1.0 for i in ITEMS)
    out, n, spent, seen = [], 0, 0.0, 0.0
    for r in room:
        seen += r
        here = []
        while n < len(ITEMS) and spent < total * seen / sum(room):
            spent += WEIGHT[ITEMS[n][0]] if ITEMS[n] else 1.0
            here.append(ITEMS[n])
            n += 1
        out.append(here)
    out[-1] += ITEMS[n:]
    return out


PLAN = spread()
TURN_AT = [PLACES * (STEPS.index((t, SUB * (t + 1) - 1)) + 1) + 2 for t in range(SPANS - 1)]
for _t, _at in enumerate(TURN_AT):
    PLAN[_at].append(("turn", _t))
SEGMENT = [i for place in PLAN for i in place] + [("turn", SPANS - 1)]
USES_MISC = ("qkv", "trans", "maxrows", "turn")


def numbered(items):
    out, n = {}, 0
    for i in items:
        if i and i[0] in USES_MISC:
            out[i] = n
            n += 1
    return out, n


FIRST_MISC, FIRST_COUNT = numbered(ITEMS)
SEG_MISC, SEG_COUNT = numbered(SEGMENT)
CHUNKS = sum(1 for i in ITEMS if i and i[0] == "max")
DIAG_NOS = [n for n, i in enumerate([i for i in ITEMS if i and i[0] == "max"]) if i[3] == i[1] // SUB]
MAX_NO = {i: n for n, i in enumerate([i for i in ITEMS if i and i[0] == "max"])}


class Segment:

    def __init__(self, a, b):
        self.a, self.b = a, b
        if a is None:
            self.misc, self.no = 0, FIRST_MISC
        elif b is None:
            self.misc = FIRST_COUNT + SEG_COUNT * a
            self.no = {("turn", t): t for t in range(SPANS)}
        else:
            self.misc, self.no = a * SEG_COUNT + FIRST_COUNT, SEG_MISC

    def before(self, item):
        return self.misc + self.no[item]

    def places(self):
        if self.a is None:
            return [ITEMS]
        if self.b is None:
            return [[i for i in place if i and i[0] == "turn"] for place in PLAN]
        return PLAN


def layer_kernel(nc, x, w_qkv, w_proj, b_proj, theta, phi, theta_noise, phi_noise, cosines, sines,
                 identity, corner, normed, heads_out, out):
    x_v = x.rearrange("b (s j p) d -> (b s) p j d", p=P, j=SUB)
    out_v = out.rearrange("b (s j p) d -> (b s) p j d", p=P, j=SUB)
    heads_v = heads_out.rearrange("(n j p) d -> n p j d", p=P, j=SUB)

    with ExitStack() as ctx:
        def sb(name, shape, dt=F32):
            return ctx.enter_context(nc.sbuf_tensor(name, shape, dt))

        def sem(name):
            return ctx.enter_context(nc.semaphore(name))

        ident = sb("ident", [P, P])
        ident_bf = sb("ident_bf", [P, P], BF16)
        diag_mask = sb("diag_mask", [P, SPAN])
        cos_t = sb("cos_t", [P, SPANS, 2 * SUB * GF])
        sin_t = sb("sin_t", [P, SPANS, 2 * SUB * GF])
        wave = sb("wave", [P, KT, 2 * DIM])
        wproj = sb("wproj", [P, KT, DIM])
        bias = sb("bias", [P, DIM])

        banks = ctx.enter_context(nc.psum_tensor("banks", [P, 8, 512], F32))
        psum = [banks[:, n, :] for n in range(8)]

        s_const = sem("const_loaded")
        s_passed = sem("waits_passed")
        s_trig_in = sem("trig_loaded")
        s_setup = sem("vector_setup")
        s_pool_setup = sem("pool_setup")
        s_xin = [sem(f"x_loaded{n}") for n in range(2)]
        s_stat = sem("stats_chain")
        s_rvar = sem("inverse_variance_ready")
        s_std = sem("inverse_deviation_ready")
        s_xn = sem("normed_ready")
        s_xt = sem("normed_turned")
        s_xte = sem("turned_copied")
        s_nout = [sem(f"normed_stored{n}") for n in range(2)]

        with ExitStack() as stage:
            def sb1(name, shape, dt=F32):
                return stage.enter_context(nc.sbuf_tensor(name, shape, dt))

            trig_a = sb1("trig_a", [P, KT, 2, DIM])
            trig_b = sb1("trig_b", [P, KT, 2, DIM])
            turns = sb1("turns", [P, KT * 2 * DIM])
            xin = sb1("xin", [P, 2, SUB, DIM])
            xn = sb1("xn", [P, 2, SUB, DIM])
            xt = sb1("xt", [P, 2, KT, SPAN])
            stats = sb1("stats", [P, SUB, 6])
            mv = sb1("mv", [P, 2, SUB, 2])
            rvar = sb1("rvar", [P, 2, SUB])
            rstd = sb1("rstd", [P, 2, SUB])

            with nc.Block() as block:
                @block.sync
                def _(sp):
                    sp.dma_start(ident[:, :], identity).then_inc(s_const, 16)
                    sp.dma_start(diag_mask[:, :], corner).then_inc(s_const, 16)
                    for src, dst, half in ((theta, trig_a, 0), (phi, trig_a, 1), (theta_noise, trig_b, 0),
                                           (phi_noise, trig_b, 1)):
                        sp.dma_start(dst[:, :, half, :], src.rearrange("(k p) n -> p k n", p=P)).then_inc(s_trig_in, 16)
                    sp.dma_start(cos_t[:, :, :], cosines).then_inc(s_const, 16)
                    sp.dma_start(sin_t[:, :, :], sines).then_inc(s_const, 16)
                    sp.dma_start(wproj[:, :, :], w_proj.rearrange("(k p) n -> p k n", p=P)).then_inc(s_const, 16)
                    sp.dma_start(bias[:, :], b_proj.rearrange("(a n) -> a n", a=1).to_broadcast([P, DIM])).then_inc(s_const, 16)
                    with sp.Fori(0, BLOCKS // 2) as it:
                        for half in range(2):
                            n = it * 2 + half
                            sp.wait_ge(s_xte, n * 2 + 2)
                            sp.dma_start(normed[n // SPANS, :, :, bass.ds((n % SPANS) * SPAN, SPAN)],
                                         xt[:, half, :, :]).then_inc(s_nout[half], 16)
                    for half in range(2):
                        sp.wait_ge(s_nout[half], 16 * (BLOCKS // 2))

                @block.gpsimd
                def _(pool):
                    pool.wait_ge(s_const, 96)
                    nc.gpsimd.tensor_copy(ident_bf[:, :], ident[:, :]).then_inc(s_pool_setup, 1)
                    for half in range(2):
                        pool.dma_start(xin[:, half, :, :], x_v[half]).then_inc(s_xin[half], 16)
                    with pool.Fori(0, BLOCKS // 2 - 1) as it:
                        for half in range(2):
                            n = it * 2 + half
                            pool.wait_ge(s_xn, n + 1)
                            pool.dma_start(xin[:, half, :, :], x_v[n + 2]).then_inc(s_xin[half], 16)

                @block.vector
                def _(dve):
                    chain = [0]

                    def link(ins):
                        chain[0] += 1
                        ins.then_inc(s_setup, 1)
                        dve.wait_ge(s_setup, chain[0])

                    two_pi = 2.0 * np.pi
                    c1 = float(np.float32(6.28125))
                    c2 = float(np.float32(two_pi - c1) - np.float32(two_pi - c1) % np.float32(2.0 ** -20))
                    c3 = float(two_pi - c1 - c2)
                    magic = float(1.5 * 2 ** 23)
                    dve.wait_ge(s_trig_in, 64)
                    flat_a = trig_a[:, :, :, :].rearrange("p k s n -> p (k s n)")
                    flat_b = trig_b[:, :, :, :].rearrange("p k s n -> p (k s n)")
                    link(nc.vector.tensor_tensor(flat_a, flat_a, flat_b, ALU.add))
                    for half in range(2):
                        view = turns[:, :].rearrange("p (k s n) -> p k s n", k=KT, s=2)[:, :, half, :]
                        link(nc.vector.tensor_scalar(view, trig_a[:, :, half, :], 1.0 / two_pi,
                                                     0.25 * (1 - half), ALU.mult, ALU.add))
                    link(nc.vector.tensor_scalar(turns[:, :], turns[:, :], magic, None, ALU.add))
                    link(nc.vector.tensor_scalar(turns[:, :], turns[:, :], -magic, None, ALU.add))
                    for c in (c1, c2, c3):
                        link(nc.vector.scalar_tensor_tensor(out=flat_a, in0=turns[:, :], scalar=-c, in1=flat_a,
                                                            op0=ALU.mult, op1=ALU.add))
                    link(nc.vector.tensor_scalar(trig_a[:, :, 0, :], trig_a[:, :, 0, :], float(np.pi / 2), None, ALU.add))
                    pi = float(np.nextafter(np.float32(np.pi), np.float32(0)))
                    link(nc.vector.tensor_scalar(flat_a, flat_a, pi, -pi, ALU.min, ALU.max))

                    assert chain[0] == REDUCE_OPS

                    def norm(n, half, loaded, reused):
                        dve.wait_ge(s_xin[half], loaded)
                        for j in range(SUB):
                            nc.vector.bn_stats(stats[:, j, :], xin[:, half, j, :]).then_inc(s_stat, 1)
                        dve.wait_ge(s_stat, n * 9 + 4)
                        dve.sem_inc(s_passed, 1)
                        for j in range(SUB):
                            dve.wait_ge(s_setup, REDUCE_OPS)
                            nc.vector.bn_aggr(mv[:, half, j, :], stats[:, j, :]).then_inc(s_stat, 1)
                        dve.wait_ge(s_stat, n * 9 + 8)
                        nc.vector.tensor_scalar(rvar[:, half, :], mv[:, half, :, 1], EPS, None, ALU.add).then_inc(s_stat, 1)
                        dve.wait_ge(s_stat, n * 9 + 9)
                        nc.vector.reciprocal(rvar[:, half, :], rvar[:, half, :]).then_inc(s_rvar, 1)
                        dve.wait_ge(s_std, n + 1)
                        if reused:
                            dve.wait_ge(s_xt, n * 2 - 2)
                        for j in range(SUB):
                            last = nc.vector.tensor_scalar(xn[:, half, j, :], xin[:, half, j, :], mv[:, half, j, 0:1],
                                                           rstd[:, half, j:j + 1], ALU.subtract, ALU.mult)
                        last.then_inc(s_xn, 1)

                    norm(0, 0, 16, False)
                    norm(1, 1, 16, False)
                    with dve.Fori(1, BLOCKS // 2) as it:
                        for half in range(2):
                            norm(it * 2 + half, half, it * 16 + 16, True)

                @block.scalar
                def _(act):
                    act.wait_ge(s_setup, REDUCE_OPS)
                    for k in range(KT):
                        nc.scalar.activation(wave[:, k, :], trig_a[:, k, :, :].rearrange("p s n -> p (s n)"),
                                             ACT.Sin)

                    def copy_out(n, half, it):
                        for k in range(KT):
                            act.wait_ge(s_xt, n * 2 + k + 1)
                            if k == 0 and it is not None:
                                act.wait_ge(s_nout[half], it * 16)
                            nc.scalar.activation(xt[:, half, k, :], psum[2 * half + k][:, :], ACT.Copy).then_inc(s_xte, 1)

                    def root(n, half):
                        act.wait_ge(s_rvar, n + 1)
                        nc.scalar.activation(rstd[:, half, :], rvar[:, half, :], ACT.Sqrt).then_inc(s_std, 1)

                    root(0, 0)
                    root(1, 1)
                    copy_out(0, 0, None)
                    root(2, 0)
                    copy_out(1, 1, None)
                    root(3, 1)
                    with act.Fori(1, BLOCKS // 2 - 1) as it:
                        for half in range(2):
                            copy_out(it * 2 + half, half, it)
                            root(it * 2 + half + 2, half)
                    for half in range(2):
                        copy_out(BLOCKS - 2 + half, half, BLOCKS // 2 - 1)

                @block.tensor
                def _(pe):
                    pe.wait_ge(s_const, 96)
                    def turn(n, half, waits):
                        pe.wait_ge(s_xn, n + 1)
                        if waits:
                            pe.wait_ge(s_xte, n * 2 - 2)
                        for k in range(KT):
                            for j in range(SUB):
                                mm = nc.tensor.transpose(psum[2 * half + k][:, j * P:(j + 1) * P],
                                                         xn[:, half, j, k * P:(k + 1) * P], ident[:, :])
                            mm.then_inc(s_xt, 1)
                    turn(0, 0, False)
                    turn(1, 1, False)
                    with pe.Fori(1, BLOCKS // 2) as it:
                        for half in range(2):
                            turn(it * 2 + half, half, True)

        with ExitStack() as stage:
            def sb2(name, shape, dt=F32):
                return stage.enter_context(nc.sbuf_tensor(name, shape, dt))

            def sem2(name):
                return stage.enter_context(nc.semaphore(name))

            xg = sb2("xg", [P, KT, SEQ])
            wg = sb2("wg", [P, KT, 3 * GF])
            raw = sb2("raw", [P, 2, SUB, GF])
            rotated = sb2("rotated", [P, 2 * SUB * GF])
            crossed = sb2("crossed", [P, 2 * SUB * GF])
            rest = sb2("rest", [P, 2, SUB * HG, HD])
            parts = sb2("parts", [P, 2, SUB * HG, SPLIT_ROWS], BF16)
            stack = [sb2(f"stack{n}", [P, 2, HG, SEQ], BF16) for n in range(2)]
            v_one = [sb2(f"v_one{n}", [P, TILES, HG, VW]) for n in range(2)]
            probs = sb2("probs", [P, 2, HG, SPAN])
            chunk_max = sb2("chunk_max", [P, SUB * HG, SPANS])
            row_max = sb2("row_max", [P, SUB, HG])
            max_rest = sb2("max_rest", [P, SUB, HG])
            max_parts = sb2("max_parts", [P, SUB, HG, MAX_ROWS], BF16)
            masked = sb2("masked", [P, 4, SPAN], BF16)
            o_raw = sb2("o_raw", [P, SPAN])
            inverse = sb2("inverse", [P, SUB * HG])
            o_norm = sb2("o_norm", [P, 2, SUB, GF])

            scores_bank = psum[0:4]
            scores_pair = [banks[:, 0:2, :], banks[:, 2:4, :]]
            max_bank = psum[4:6]
            misc = psum[6]
            out_bank = psum[7]
            misc_bf = misc.bitcast(BF16)

            s_xg = sem2("unit_input_loaded")
            s_vset = sem2("v_ones_set")
            s_scores = sem2("scores_ready")
            s_exp = sem2("exp_done")
            s_masked = sem2("diagonal_masked")
            s_av = sem2("values_summed")
            s_ocopy = sem2("output_copied")
            s_inv = sem2("denominators_inverted")
            s_ostore = [sem2(f"output_stored{n}") for n in range(2)]
            s_filled = sem2("misc_filled")
            s_emptied = sem2("misc_emptied")
            s_rope = sem2("rope_chain")
            s_chunk = sem2("chunk_scored")
            s_read = sem2("chunk_reduced")
            s_msplit = sem2("maximum_split")

            def stack_parity(u_parity):
                return stack[u_parity], v_one[u_parity]

            N_EXP = 2 * NSTEP
            N_MSPLIT = 5 * SPANS
            N_ROPE = ROPE_OPS * SPANS

            def segments(engine, run):
                run(Segment(None, 0), 0)
                with engine.Fori(0, UNITS // 2 - 1) as it:
                    for half in range(2):
                        run(Segment(it * 2 + half, it * 2 + half + 1), half)
                run(Segment(UNITS - 2, UNITS - 1), 0)
                run(Segment(UNITS - 1, None), 1)

            def rope(eng, unit, seg, i):
                _, c, n = i
                if (unit is nc.vector) != (n in (4, 5, 8, 9)):
                    return
                done = seg.b * N_ROPE + ROPE_OPS * c + n
                if not (isinstance(done, int) and done == 0):
                    eng.wait_ge(s_rope, done)
                if n < 4:
                    flat = raw[:, :, :, :].rearrange("p s j n -> p (s j n)")
                    if n == 0:
                        eng.wait_ge(s_emptied, seg.before(("qkv", c, 1)) + 1)
                        ins = unit.tensor_tensor(rotated[:, :], flat, cos_t[:, c, :], ALU.mult)
                    elif n < 3:
                        e = n - 1
                        halves = flat.rearrange("p (a e d) -> p a e d", e=2, d=HD // 2)
                        sines_h = sin_t[:, c, :].rearrange("p (a e d) -> p a e d", e=2, d=HD // 2)
                        crossed_h = crossed[:, :].rearrange("p (a e d) -> p a e d", e=2, d=HD // 2)
                        ins = unit.tensor_tensor(crossed_h[:, :, e, :], halves[:, :, 1 - e, :], sines_h[:, :, e, :], ALU.mult)
                    else:
                        ins = unit.tensor_tensor(rotated[:, :], rotated[:, :], crossed[:, :], ALU.add)
                    ins.then_inc(s_rope, 1)
                    return
                k, s = (n - 4) // 2, n % 2
                if n == 4 and c > 0:
                    eng.wait_ge(s_filled, seg.before(("trans", SUB * c - 1)) + 1)
                value = rotated[:, :].rearrange("p (s a d) -> p s a d", s=2, d=HD)[:, s, :, :]
                left = rest[:, s, :, :]
                by_slot = parts[:, s, :, :].rearrange("p a (m d) -> p a m d", d=HD)
                first, last, step = (Q_SLOTS, K_SLOTS)[s][(0, 0, 1, 1)[k]]
                if k % 2 == 0:
                    src = (value, None, left)[k].unsqueeze(2)
                    count = len(range(first, last, step))
                    ins = unit.tensor_copy(by_slot[:, :, first:last:step, :], src.to_broadcast([P, SUB * HG, count, HD]))
                else:
                    dst = left if k == 1 else by_slot[:, :, (Q_SLOTS, K_SLOTS)[s][2][0], :]
                    ins = unit.tensor_tensor(dst, (value if k == 1 else left), by_slot[:, :, first, :], ALU.subtract)
                ins.then_inc(s_rope, 1)

            with nc.Block() as block:
                @block.sync
                def _(sp):
                    def load(u):
                        sp.dma_start(xg[:, :, :], normed[u // GROUPS]).then_inc(s_xg, 16)
                        sp.dma_start(wg[:, :, :], w_qkv[u % GROUPS]).then_inc(s_xg, 16)

                    def store(seg, t):
                        u = seg.a
                        sp.wait_ge(s_emptied, seg.before(("turn", t)) + 1)
                        sp.dma_start(heads_v[(u // GROUPS) * SPANS + t, :, :, bass.ds((u % GROUPS) * GF, GF)],
                                     o_norm[:, t % 2, :, :]).then_inc(s_ostore[t % 2], 16)

                    load(0)

                    def run(seg, parity):
                        if seg.a is None:
                            sp.wait_ge(s_filled, seg.before(("qkv", SPANS - 1, 1)) + 1)
                            load(1)
                            return
                        for t in range(SPANS):
                            store(seg, t)
                            if t == 2 and seg.b is not None and not (isinstance(seg.b, int) and seg.b == UNITS - 1):
                                sp.wait_ge(s_filled, seg.before(("qkv", SPANS - 1, 1)) + 1)
                                load(seg.b + 1)

                    segments(sp, run)
                    for n in range(2):
                        sp.wait_ge(s_ostore[n], 16 + 16 * (UNITS * SPANS // 2))

                @block.tensor
                def _(pe):
                    def item(seg, i, qk, v1):
                        if i is None or i[0] == "rope":
                            return
                        kind = i[0]
                        if kind in USES_MISC:
                            n = seg.before(i)
                            if not (isinstance(n, int) and n == 0):
                                pe.wait_ge(s_emptied, n)
                        if kind == "qkv":
                            _, c, pair = i
                            if c == 0 and pair == 0:
                                pe.wait_ge(s_xg, (seg.b + 1) * 32)
                            for j in range(2):
                                tile = SUB * c + 2 * pair + j
                                for k in range(KT):
                                    mm = nc.tensor.matmul(misc[:, j * 3 * GF:(j + 1) * 3 * GF], xg[:, k, tile * P:(tile + 1) * P],
                                                          wg[:, k, :], start=(k == 0), stop=(k == KT - 1))
                            mm.then_inc(s_filled, 1)
                        elif kind == "trans":
                            c, j = i[1] // SUB, i[1] % SUB
                            if j == 0:
                                pe.wait_ge(s_rope, seg.b * N_ROPE + ROPE_OPS * (c + 1))
                            for s in range(2):
                                for h in range(HG):
                                    at = (s * HG + h) * P
                                    mm = nc.tensor.transpose(misc_bf[0:SPLIT_ROWS, at:at + P], parts[:, s, j * HG + h, :], ident_bf[:, :])
                            mm.then_inc(s_filled, 1)
                        elif kind == "max":
                            _, tile, h, c = i
                            n = MAX_NO[i]
                            if h == 0 and c == 0 and tile % SUB == 0:
                                pe.wait_ge(s_emptied, seg.before(("trans", tile + SUB - 1)) + 1)
                            if n >= 2:
                                pe.wait_ge(s_read, seg.b * CHUNKS + n - 1)
                            wide = SPAN if c < tile // SUB else P * (tile % SUB + 1)
                            nc.tensor.matmul(max_bank[n % 2][:, 0:wide], qk[0:SPLIT_ROWS, 0, h, tile * P:(tile + 1) * P],
                                             qk[0:SPLIT_ROWS, 1, h, c * SPAN:c * SPAN + wide],
                                             start=True, stop=True).then_inc(s_chunk, 1)
                        elif kind == "maxrows":
                            _, t, half = i
                            if half == 0:
                                pe.wait_ge(s_msplit, seg.b * N_MSPLIT + 5 * (t + 1))
                            for h in range(HG):
                                for j in range(2):
                                    at = (h * 2 + j) * P
                                    mm = nc.tensor.transpose(misc_bf[SPLIT_ROWS:P, at:at + P],
                                                             max_parts[:, 2 * half + j, h, :], ident_bf[:, :])
                            mm.then_inc(s_filled, 1)
                        elif kind == "turn":
                            t = i[1]
                            pe.wait_ge(s_ocopy, seg.a * SPANS + t + 1)
                            for j in range(SUB):
                                mm = nc.tensor.transpose(misc[:, j * P:(j + 1) * P], o_raw[:, j * P:(j + 1) * P], ident[:, :])
                            mm.then_inc(s_filled, 1)

                    def scores(seg, s, pair, qk):
                        t, j = STEPS[s]
                        w0 = widths(s)
                        if s > 0:
                            pe.wait_ge(s_exp, seg.a * N_EXP + 2 * (s - 1) + pair + 1)
                        for h in (2 * pair, 2 * pair + 1):
                            mm = nc.tensor.matmul(scores_bank[h][:, w0:SPAN], qk[:, 1, h, j * P:(j + 1) * P],
                                                  qk[:, 0, h, t * SPAN + w0:(t + 1) * SPAN], start=True, stop=True)
                        mm.then_inc(s_scores, 1)

                    def values(seg, s, v1):
                        t, j = STEPS[s]
                        w0 = widths(s)
                        pe.wait_ge(s_exp, seg.a * N_EXP + 2 * s + 2)
                        if j >= SUB * t:
                            pe.wait_ge(s_masked, seg.a * DIAG + SUB * t + (j - SUB * t) + 1)
                        if j == 0 and t > 0:
                            pe.wait_ge(s_ocopy, seg.a * SPANS + t)
                        for h in range(HG):
                            mm = nc.tensor.matmul(out_bank[VW * h:VW * (h + 1), w0:SPAN], v1[:, j, h, :],
                                                  probs[:, s % 2, h, w0:SPAN],
                                                  start=(j == 0), stop=(j == SUB * (t + 1) - 1))
                        mm.then_inc(s_av, 1)

                    def run(seg, parity):
                        mine, other = (stack_parity(parity), stack_parity(1 - parity))
                        if seg.a is None:
                            for i in ITEMS:
                                item(seg, i, *mine)
                            return
                        pe.wait_ge(s_emptied, seg.misc)
                        places = seg.places()
                        scores(seg, 0, 0, mine[0])
                        scores(seg, 0, 1, mine[0])
                        for s in range(NSTEP):
                            for place in range(PLACES):
                                if place < 2 and s + 1 < NSTEP:
                                    scores(seg, s + 1, place, mine[0])
                                elif place == 2:
                                    values(seg, s, mine[1])
                                for i in places[PLACES * s + place]:
                                    item(seg, i, *other)
                        item(seg, ("turn", SPANS - 1), *other)

                    pe.wait_ge(s_vset, 2)
                    segments(pe, run)

                @block.scalar
                def _(act):
                    def item(seg, i, qk, v1):
                        if i is None or i[0] not in ("qkv", "trans", "maxrows"):
                            return
                        kind = i[0]
                        act.wait_ge(s_filled, seg.before(i) + 1)
                        if kind == "qkv":
                            _, c, pair = i
                            if c > 0 and pair == 0:
                                act.wait_ge(s_rope, seg.b * N_ROPE + ROPE_OPS * (c - 1) + 3)
                            both = misc[:, 0:6 * GF].rearrange("p (j n) -> p j n", j=2)
                            tile = SUB * c + 2 * pair
                            nc.scalar.activation(raw[:, :, 2 * pair:2 * pair + 2, :],
                                                 both[:, :, 0:2 * GF].rearrange("p j (s n) -> p s j n", s=2), ACT.Copy)
                            nc.scalar.activation(v1[:, tile:tile + 2, :, 0:HD],
                                                 both[:, :, 2 * GF:3 * GF].rearrange("p j (h d) -> p j h d", h=HG),
                                                 ACT.Copy).then_inc(s_emptied, 1)
                        elif kind == "trans":
                            tile = i[1]
                            nc.scalar.activation(qk[0:SPLIT_ROWS, :, :, tile * P:(tile + 1) * P].rearrange("p s h n -> p (s h) n"),
                                                 misc_bf[0:SPLIT_ROWS, :].rearrange("p (a n) -> p a n", n=P),
                                                 ACT.Copy).then_inc(s_emptied, 1)
                        else:
                            _, t, half = i
                            tile = SUB * t + 2 * half
                            nc.scalar.activation(qk[SPLIT_ROWS:P, 0, :, tile * P:(tile + 2) * P],
                                                 misc_bf[SPLIT_ROWS:P, :].rearrange("p (h n) -> p h n", h=HG),
                                                 ACT.Copy).then_inc(s_emptied, 1)

                    def exps(seg, s, pair):
                        w0 = widths(s)
                        act.wait_ge(s_scores, seg.a * N_EXP + 2 * s + pair + 1)
                        if s >= 2 and pair == 0:
                            act.wait_ge(s_av, seg.a * NSTEP + s - 1)
                        src = scores_pair[pair][:, :, w0:SPAN]
                        nc.scalar.activation(probs[:, s % 2, 2 * pair:2 * pair + 2, w0:SPAN], src, ACT.Exp).then_inc(s_exp, 1)

                    def run(seg, parity):
                        mine, other = (stack_parity(parity), stack_parity(1 - parity))
                        if seg.a is None:
                            for i in ITEMS:
                                item(seg, i, *mine)
                            return
                        places = seg.places()
                        exps(seg, 0, 0)
                        exps(seg, 0, 1)
                        for s in range(NSTEP):
                            t, j = STEPS[s]
                            for place in range(PLACES):
                                if place < 2 and s + 1 < NSTEP:
                                    exps(seg, s + 1, place)
                                elif place == 2 and j == SUB * (t + 1) - 1:
                                    act.wait_ge(s_av, seg.a * NSTEP + s + 1)
                                    act.wait_ge(s_filled, seg.before(("turn", t - 1)) + 1 if t else seg.misc)
                                    nc.scalar.activation(o_raw[:, :], out_bank[:, :], ACT.Copy).then_inc(s_ocopy, 1)
                                for i in places[PLACES * s + place]:
                                    item(seg, i, *other)

                    act.wait_ge(s_vset, 2)
                    segments(act, run)

                @block.vector
                def _(dve):
                    def item(seg, i):
                        if i is None:
                            return
                        kind = i[0]
                        if kind == "max":
                            _, tile, h, c = i
                            n = MAX_NO[i]
                            dve.wait_ge(s_chunk, seg.b * CHUNKS + n + 1)
                            bank = max_bank[n % 2]
                            row = (tile % SUB) * HG + h
                            to = chunk_max[:, row, c:c + 1]
                            if c < tile // SUB:
                                ins = nc.vector.tensor_reduce(to, bank[:, :], AX.X, ALU.max)
                            else:
                                wide = P * (tile % SUB + 1)
                                d = DIAG_NOS.index(n)
                                if d >= 4:
                                    dve.wait_ge(s_read, seg.b * CHUNKS + DIAG_NOS[d - 4] + 1)
                                dve.sem_inc(s_passed, 1)
                                ins = nc.vector.tensor_tensor_reduce(
                                    out=masked[:, d % 4, 0:wide], in0=bank[:, 0:wide], in1=diag_mask[:, SPAN - wide:SPAN],
                                    scale=1.0, scalar=NEG, op0=ALU.add, op1=ALU.max, accum_out=to)
                            ins.then_inc(s_read, 1)
                            if tile % SUB == SUB - 1 and h == HG - 1 and c == tile // SUB:
                                maximum(seg, tile // SUB, n)
                        elif kind == "rope":
                            rope(dve, nc.vector, seg, i)
                        elif kind == "turn":
                            normalise(seg, i)

                    def maximum(seg, t, n):
                        base = seg.b * N_MSPLIT + 5 * t
                        dve.wait_ge(s_read, seg.b * CHUNKS + n + 1)
                        flat = row_max[:, :, :].rearrange("p j h -> p (j h)")
                        nc.vector.tensor_reduce(flat, chunk_max[:, :, 0:t + 1], AX.X, ALU.max).then_inc(s_msplit, 1)
                        dve.wait_ge(s_msplit, base + 1)
                        if t > 0:
                            dve.wait_ge(s_filled, seg.before(("maxrows", t - 1, 1)) + 1)
                        nc.vector.tensor_scalar(max_parts[:, :, :, 0], row_max[:, :, :], -1.0, None, ALU.mult).then_inc(s_msplit, 1)
                        dve.wait_ge(s_msplit, base + 2)
                        nc.vector.scalar_tensor_tensor(out=max_rest[:, :, :], in0=row_max[:, :, :], scalar=-1.0,
                                                       in1=max_parts[:, :, :, 0], op0=ALU.mult, op1=ALU.subtract).then_inc(s_msplit, 1)
                        dve.wait_ge(s_msplit, base + 3)
                        nc.vector.tensor_copy(max_parts[:, :, :, 1], max_rest[:, :, :]).then_inc(s_msplit, 1)
                        dve.wait_ge(s_msplit, base + 4)
                        nc.vector.tensor_tensor(max_parts[:, :, :, 2], max_rest[:, :, :], max_parts[:, :, :, 1],
                                                ALU.subtract).then_inc(s_msplit, 1)

                    def normalise(seg, i):
                        t = i[1]
                        n = seg.a * SPANS + t
                        dve.wait_ge(s_filled, seg.before(i) + 1)
                        turned = misc.rearrange("p (a d) -> p a d", d=VW)
                        nc.vector.reciprocal(inverse[:, :], turned[:, :, HD]).then_inc(s_inv, 1)
                        dve.wait_ge(s_inv, n + 1)
                        dve.wait_ge(s_ostore[t % 2], seg.a * 32 + 16 * (t // 2) + 16)
                        nc.vector.tensor_tensor(
                            o_norm[:, t % 2, :, :].rearrange("p j (h d) -> p (j h) d", h=HG),
                            misc.rearrange("p (a d) -> p a d", d=VW)[:, :, 0:HD],
                            inverse[:, :].unsqueeze(2).to_broadcast([P, SUB * HG, HD]),
                            ALU.mult).then_inc(s_emptied, 1)

                    def run(seg, parity):
                        for place in seg.places():
                            for i in place:
                                item(seg, i)
                        if seg.a is not None:
                            item(seg, ("turn", SPANS - 1))

                    nc.vector.memset(max_parts[:, :, :, :], 0.0)
                    for n in range(2):
                        nc.vector.memset(inverse[:, n:n + 1], 0.0).then_inc(s_ostore[n], 16)
                    for n in range(2):
                        nc.vector.memset(stack[n][SPLIT_ROWS:P, 1, :, :], 1.0)
                        nc.vector.memset(v_one[n][:, :, :, HD:VW], 1.0).then_inc(s_vset, 1)
                    segments(dve, run)

                @block.gpsimd
                def _(pool):
                    def item(seg, i):
                        if i and i[0] == "rope":
                            rope(pool, nc.gpsimd, seg, i)

                    def mask(seg, s):
                        t, j = STEPS[s]
                        if j < SUB * t:
                            return
                        w0 = widths(s)
                        pool.wait_ge(s_exp, seg.a * N_EXP + 2 * s + 2)
                        pool.sem_inc(s_passed, 1)
                        square = probs[:, s % 2, :, w0:w0 + P]
                        nc.gpsimd.affine_select(out=square, in_=square, compare_op=ALU.is_ge, fill=0.0, base=0,
                                                pattern=[[0, HG], [1, P]], channel_multiplier=-1).then_inc(s_masked, 1)

                    def run(seg, parity):
                        if seg.a is not None:
                            mask(seg, 0)
                        for n, place in enumerate(seg.places()):
                            if seg.a is not None and n % PLACES == 1 and n // PLACES + 1 < NSTEP:
                                mask(seg, n // PLACES + 1)
                            for i in place:
                                item(seg, i)

                    segments(pool, run)

        with ExitStack() as stage:
            def sb3(name, shape, dt=F32):
                return stage.enter_context(nc.sbuf_tensor(name, shape, dt))

            def sem3(name):
                return stage.enter_context(nc.semaphore(name))

            heads3 = sb3("heads3", [P, 2, SUB, DIM])
            x3 = sb3("x3", [P, 2, SUB, DIM])
            heads_t = sb3("heads_t", [P, SUB, KT * P])
            mid = sb3("mid", [P, 2, SUB, DIM])
            xn3 = sb3("xn3", [P, SUB, DIM])
            xn_t = sb3("xn_t", [P, SUB, KT * P])
            squares = sb3("squares", [P, SUB, 2 * DIM])
            power = sb3("power", [P, SUB, DIM])
            result = sb3("result", [P, 2, SUB, DIM])
            stats3 = sb3("stats3", [P, SUB, 6])
            mv3 = sb3("mv3", [P, SUB, 2])
            rvar3 = sb3("rvar3", [P, SUB])
            rstd3 = sb3("rstd3", [P, SUB])
            token = sb3("token", [P, 8])

            heads_banks = banks[:, 0:2, :].rearrange("p a (b n) -> p (a b) n", b=2)
            proj_banks = banks[:, 2:4, :].rearrange("p a (b n) -> p (a b) n", b=2)
            xn_banks = banks[:, 4:6, :].rearrange("p a (b n) -> p (a b) n", b=2)
            wave_banks = psum[6:8]

            s_load = [sem3(f"block_loaded{n}") for n in range(2)]
            s_bias = sem3("bias_added")
            s_ht = sem3("heads_turned")
            s_htc = sem3("heads_copied")
            s_proj = sem3("projected")
            s_mid = sem3("residual_added")
            s_st = sem3("stats3_chain")
            s_rv = sem3("inverse_variance3_ready")
            s_sd = sem3("inverse_deviation3_ready")
            s_xn3 = sem3("normed3_ready")
            s_nt = sem3("normed3_turned")
            s_ntc = sem3("normed3_copied")
            s_wave = sem3("waves_ready")
            s_sq = sem3("squares_ready")
            s_pow = sem3("power_ready")
            s_mod = sem3("modulus_ready")
            s_res = sem3("result_ready")
            s_store = [sem3(f"result_stored{n}") for n in range(2)]

            def first(n):
                return isinstance(n, int) and n == 0

            with nc.Block() as block:
                @block.sync
                def _(sp):
                    def load(n, half):
                        sp.dma_start(heads3[:, half, :, :], heads_v[n]).then_inc(s_load[half], 16)
                        sp.dma_start(x3[:, half, :, :], x_v[n]).then_inc(s_load[half], 16)

                    def store(n, half):
                        sp.wait_ge(s_res, n + 2)
                        sp.dma_start(out_v[n], result[:, half, :, :]).then_inc(s_store[half], 16)

                    load(0, 0)
                    load(1, 1)
                    with sp.Fori(0, BLOCKS // 2 - 1) as it:
                        for half in range(2):
                            n = it * 2 + half
                            sp.wait_ge(s_ht, n * 2 + 2)
                            sp.wait_ge(s_mid, n * 2 + 2)
                            load(n + 2, half)
                            store(n, half)
                    store(BLOCKS - 2, 0)
                    store(BLOCKS - 1, 1)
                    for half in range(2):
                        sp.wait_ge(s_store[half], 16 + 16 * (BLOCKS // 2))

                @block.tensor
                def _(pe):
                    def front(n, half, count):
                        pe.wait_ge(s_load[half], count * 32 + 32)
                        if not first(n):
                            pe.wait_ge(s_htc, n * 2)
                        for j in range(SUB):
                            for k in range(KT):
                                mm = nc.tensor.transpose(heads_banks[:, j, k * P:(k + 1) * P],
                                                         heads3[:, half, j, k * P:(k + 1) * P], ident[:, :])
                            if j % 2:
                                mm.then_inc(s_ht, 1)

                    def project(n):
                        if not first(n):
                            pe.wait_ge(s_mid, n * 2)
                        for j in range(SUB):
                            if j % 2 == 0:
                                pe.wait_ge(s_htc, n * 2 + j // 2 + 1)
                            for k in range(KT):
                                mm = nc.tensor.matmul(proj_banks[:, j, :], heads_t[:, j, k * P:(k + 1) * P], wproj[:, k, :],
                                                      start=(k == 0), stop=(k == KT - 1))
                            if j % 2:
                                mm.then_inc(s_proj, 1)

                    def turn(n):
                        pe.wait_ge(s_xn3, n + 1)
                        pe.wait_ge(s_ntc, n * 2 + 1)
                        for j in range(SUB):
                            for k in range(KT):
                                mm = nc.tensor.transpose(xn_banks[:, j, k * P:(k + 1) * P], xn3[:, j, k * P:(k + 1) * P],
                                                         ident[:, :])
                            if j % 2:
                                mm.then_inc(s_nt, 1)

                    def waves(n):
                        for j in range(SUB):
                            if j % 2 == 0:
                                pe.wait_ge(s_ntc, n * 2 + j // 2 + 2)
                            pe.wait_ge(s_sq, n * SUB + j + 1)
                            for k in range(KT):
                                mm = nc.tensor.matmul(wave_banks[j % 2], xn_t[:, j, k * P:(k + 1) * P], wave[:, k, :],
                                                      start=(k == 0), stop=(k == KT - 1))
                            mm.then_inc(s_wave, 1)

                    def front_only(n, half, count):
                        front(n, half, count)
                        project(n)

                    def step(n, half, count, has_next):
                        if has_next:
                            front(n + 1, 1 - half, count + half)
                        turn(n)
                        if has_next:
                            project(n + 1)
                        waves(n)

                    front_only(0, 0, 0)
                    with pe.Fori(0, BLOCKS // 2 - 1) as it:
                        for half in range(2):
                            step(it * 2 + half, half, it, True)
                    step(BLOCKS - 2, 0, BLOCKS // 2 - 1, True)
                    step(BLOCKS - 1, 1, BLOCKS // 2 - 1, False)

                @block.scalar
                def _(act):
                    def front(n):
                        for a in range(2):
                            act.wait_ge(s_ht, n * 2 + a + 1)
                            if a == 0 and not first(n):
                                act.wait_ge(s_proj, n * 2)
                            nc.scalar.activation(heads_t[:, 2 * a:2 * a + 2, :], heads_banks[:, 2 * a:2 * a + 2, :],
                                                 ACT.Copy).then_inc(s_htc, 1)

                    def root(n):
                        act.wait_ge(s_rv, n + 1)
                        nc.scalar.activation(rstd3[:, :], rvar3[:, :], ACT.Sqrt).then_inc(s_sd, 1)

                    def back(n):
                        for a in range(2):
                            act.wait_ge(s_nt, n * 2 + a + 1)
                            if a == 0:
                                act.wait_ge(s_wave, n * SUB + 1)
                            nc.scalar.activation(xn_t[:, 2 * a:2 * a + 2, :], xn_banks[:, 2 * a:2 * a + 2, :],
                                                 ACT.Copy).then_inc(s_ntc, 1)
                        for j in range(SUB):
                            if j == 0:
                                act.wait_ge(s_pow, n * 2 + 1)
                            act.wait_ge(s_wave, n * SUB + j + 2)
                            nc.scalar.activation(squares[:, j, :], wave_banks[j % 2], ACT.Square).then_inc(s_sq, 1)

                    def modulus(n, half, count):
                        act.wait_ge(s_pow, n * 2 + 3)
                        act.wait_ge(s_store[half], count * 16 + 16)
                        nc.scalar.activation(result[:, half, :, :], power[:, :, :], ACT.Sqrt).then_inc(s_mod, 1)

                    def step(n, half, count, has_next):
                        if has_next:
                            front(n + 1)
                        back(n)
                        if has_next:
                            root(n + 1)
                        modulus(n, half, count)

                    act.wait_ge(s_mod, 1)
                    front(0)
                    root(0)
                    with act.Fori(0, BLOCKS // 2 - 1) as it:
                        for half in range(2):
                            step(it * 2 + half, half, it, True)
                    step(BLOCKS - 2, 0, BLOCKS // 2 - 1, True)
                    step(BLOCKS - 1, 1, BLOCKS // 2 - 1, False)

                @block.vector
                def _(dve):
                    for a, (s, n) in enumerate(((s_ntc, 1), (s_sq, 2), (s_wave, 1), (s_pow, 1), (s_res, 1), (s_store[0], 16),
                                                (s_store[1], 16), (s_mod, 1))):
                        nc.vector.memset(token[:, a:a + 1], 0.0).then_inc(s, n)

                    def front(n, half):
                        dve.wait_ge(s_bias, n + 1)
                        if not first(n):
                            dve.wait_ge(s_res, n)
                        for a in range(2):
                            dve.wait_ge(s_proj, n * 2 + a + 1)
                            nc.vector.tensor_tensor(mid[:, half, 2 * a:2 * a + 2, :], proj_banks[:, 2 * a:2 * a + 2, :],
                                                    x3[:, half, 2 * a:2 * a + 2, :], ALU.add).then_inc(s_mid, 1)
                        for j in range(SUB):
                            if j % 2 == 0:
                                dve.wait_ge(s_mid, n * 2 + j // 2 + 1)
                            nc.vector.bn_stats(stats3[:, j, :], mid[:, half, j, :]).then_inc(s_st, 1)
                        dve.wait_ge(s_st, n * 9 + 4)
                        dve.sem_inc(s_passed, 1)
                        for j in range(SUB):
                            nc.vector.bn_aggr(mv3[:, j, :], stats3[:, j, :]).then_inc(s_st, 1)
                        dve.wait_ge(s_st, n * 9 + 8)
                        nc.vector.tensor_scalar(rvar3[:, :], mv3[:, :, 1], EPS, None, ALU.add).then_inc(s_st, 1)
                        dve.wait_ge(s_st, n * 9 + 9)
                        nc.vector.reciprocal(rvar3[:, :], rvar3[:, :]).then_inc(s_rv, 1)
                        dve.wait_ge(s_sd, n + 1)
                        if not first(n):
                            dve.wait_ge(s_nt, n * 2)
                        for j in range(SUB):
                            last = nc.vector.tensor_scalar(xn3[:, j, :], mid[:, half, j, :], mv3[:, j, 0:1],
                                                           rstd3[:, j:j + 1], ALU.subtract, ALU.mult)
                        last.then_inc(s_xn3, 1)

                    front(0, 0)
                    with dve.Fori(0, BLOCKS // 2 - 1) as it:
                        for half in range(2):
                            front(it * 2 + half + 1, 1 - half)
                    front(BLOCKS - 1, 1)

                @block.gpsimd
                def _(pool):
                    def front(n, half, count):
                        pool.wait_ge(s_load[half], count * 32 + 32)
                        nc.gpsimd.tensor_tensor(x3[:, half, :, :], x3[:, half, :, :],
                                                bias[:, :].unsqueeze(1).to_broadcast([P, SUB, DIM]), ALU.add).then_inc(s_bias, 1)

                    def back(n, half):
                        pool.wait_ge(s_mod, n + 1)
                        for a in range(2):
                            pool.wait_ge(s_sq, n * SUB + 2 * a + 4)
                            nc.gpsimd.tensor_tensor(power[:, 2 * a:2 * a + 2, :], squares[:, 2 * a:2 * a + 2, 0:DIM],
                                                    squares[:, 2 * a:2 * a + 2, DIM:2 * DIM], ALU.add).then_inc(s_pow, 1)
                        pool.wait_ge(s_mod, n + 2)
                        nc.gpsimd.tensor_tensor(result[:, half, :, :], result[:, half, :, :], mid[:, half, :, :],
                                                ALU.add).then_inc(s_res, 1)

                    pool.wait_ge(s_mod, 1)
                    front(0, 0, 0)
                    with pool.Fori(0, BLOCKS // 2 - 1) as it:
                        for half in range(2):
                            front(it * 2 + half + 1, 1 - half, it + half)
                            back(it * 2 + half, half)
                    front(BLOCKS - 1, 1, BLOCKS // 2 - 1)
                    back(BLOCKS - 2, 0)
                    back(BLOCKS - 1, 1)


def tables():
    inv = (np.float32(1.0) / np.float32(10000.0) ** (np.arange(0, HD, 2, dtype=np.float32) / np.float32(HD))).astype(np.float32)
    angle = np.arange(SEQ, dtype=np.float32)[:, None] * inv[None, :]
    cos, sin = np.cos(angle).astype(np.float32), np.sin(angle).astype(np.float32)
    cos, sin = np.concatenate([cos, cos], 1), np.concatenate([-sin, sin], 1)
    scale = np.array([HD ** -0.5, 1.0], np.float32)

    def lay(t):
        t = t.reshape(SPANS, SUB, P, 1, HD).transpose(2, 0, 1, 3, 4)
        t = np.broadcast_to(t[:, :, None], (P, SPANS, 2, SUB, HG, HD)) * scale[None, None, :, None, None, None]
        return np.ascontiguousarray(t.reshape(P, SPANS, 2 * SUB * GF).astype(np.float32))

    corner = np.zeros((P, SPAN), np.float32)
    corner[:, SPAN - P:] = np.where(np.arange(P)[None, :] > np.arange(P)[:, None], np.float32(NEG), np.float32(0))
    return lay(cos), lay(sin), np.eye(P, dtype=np.float32), corner


def kernel(L0_attn_x, L0_attn_w_qkv, L0_attn_w_proj, L0_attn_b_proj, L0_ffn_theta, L0_ffn_phi,
           L0_ffn_theta_noise, L0_ffn_phi_noise):
    import concourse.bacc as bacc
    from concourse.bass_utils import run_bass_kernel_spmd

    cosines, sines, eye, corner = tables()
    w_qkv = np.asarray(L0_attn_w_qkv).reshape(KT, P, 3, GROUPS, GF).transpose(3, 1, 0, 2, 4).reshape(GROUPS, P, KT, 3 * GF)
    arrays = {
        "x": L0_attn_x, "w_qkv": w_qkv, "w_proj": L0_attn_w_proj, "b_proj": L0_attn_b_proj,
        "theta": L0_ffn_theta, "phi": L0_ffn_phi, "theta_noise": L0_ffn_theta_noise, "phi_noise": L0_ffn_phi_noise,
        "cosines": cosines, "sines": sines, "eye": eye, "corner": corner,
    }
    arrays = {name: np.ascontiguousarray(a) for name, a in arrays.items()}
    nc = bacc.Bacc("TRN2", target_bir_lowering=False, num_devices=1)
    args = [nc.dram_tensor(name, a.shape, F32, kind="ExternalInput").ap() for name, a in arrays.items()]
    normed = nc.dram_tensor("normed", [BATCH, P, KT, SEQ], F32, kind="Internal").ap()
    heads_out = nc.dram_tensor("heads_out", [BATCH * SEQ, DIM], F32, kind="Internal").ap()
    out = nc.dram_tensor("out", [BATCH, SEQ, DIM], F32, kind="ExternalOutput").ap()
    layer_kernel(nc, *args, normed, heads_out, out)
    return run_bass_kernel_spmd(nc, [arrays], core_ids=[0]).results[0]["out"]
```

```python
from contextlib import ExitStack

import numpy as np

import concourse.bass as bass
from concourse import mybir
from concourse.alu_op_type import AluOpType as ALU

ACT = mybir.ActivationFunctionType
AX = mybir.AxisListType
F32 = mybir.dt.float32
BF16 = mybir.dt.bfloat16

P = 128
BATCH, SEQ, DIM, HEADS = 4, 2048, 256, 16
HD = DIM // HEADS
HG = 4
GROUPS = HEADS // HG
UNITS = BATCH * GROUPS
KT = DIM // P
SPAN = 512
SPANS = SEQ // SPAN
SUB = SPAN // P
TILES = SEQ // P
BLOCKS = BATCH * SPANS
GF = HG * HD
VW = 32
EPS = 1e-5

PARTS = 6
SPLIT_ROWS = PARTS * HD
Q_SLOTS = [(0, 3, 1), (3, 6, 2), (4, 5, 1)]
K_SLOTS = [(2, 5, 1), (1, 6, 4), (0, 1, 1)]
MAX_ROWS = P - SPLIT_ROWS
NEG = -1e30

ROPE_OPS = 12
REDUCE_OPS = 10


def share(item):
    return 1.0 if item[4] < item[2] // SUB else (item[2] % SUB + 1) / SUB


def vector_us(item):
    return 0.07 + 0.53 * share(item) if item[0] == "max" else 0.0


def project(d, c):
    return [("qkv", d, c, 0), ("qkv", d, c, 1)] + [("rope", d, c, n) for n in range(ROPE_OPS)]


def maxima(t):
    return [("max", 1, SUB * t + j, h, c) for j in range(SUB) for h in range(HG) for c in range(t + 1)]


AHEAD = [((1, 2), 0.01, 0.17), ((1, 3), 0.20, 0.25), ((2, 0), 0.48, 0.24), ((2, 1), 0.74, 0.24)]


def preparation():
    timed, now = [], 0.0

    def lay(items):
        nonlocal now
        for i in items:
            timed.append((now, i))
            now += 1.0 if i in head else vector_us(i)

    head = [("trans", 1, j) for j in range(SUB)]
    lay(head)
    for t in range(SPANS):
        chunks = maxima(t)
        trans = [("trans", 1, SUB * (t + 1) + j) for j in range(SUB)] if t + 1 < SPANS else []
        rows = [("maxrows", 1, t - 1, 0), ("maxrows", 1, t - 1, 1)] if t else []
        for n, i in enumerate(chunks):
            lay([i])
            if n in (4, 7) and rows:
                lay([rows.pop(0)])
            if trans and (n + 1 - len(chunks) // 4) * 5 > (SUB + 1 - len(trans)) * (len(chunks) * 3 // 4):
                lay([trans.pop(0)])
        lay(trans)
    for (d, c), start, length in AHEAD:
        items = project(d, c)
        for n, i in enumerate(items):
            at = start + (length * (n + 1) / len(items) if i[0] == "rope" else 0.02 * n)
            timed.append((now * at, i))
    timed += [(0.0, LATE[0]), (0.01 * now, LATE[1])]
    return sorted(((at / now * FULL, i) for at, i in timed), key=lambda p: p[0])


FULL = 1.005
LATE = [("maxrows", 0, SPANS - 1, 0), ("maxrows", 0, SPANS - 1, 1)]
ITEMS = preparation()
STEPS = [(t, j) for t in range(SPANS) for j in range(SUB * (t + 1))]
NSTEP = len(STEPS)
DIAG = SUB * SPANS
PLACES = 5


def widths(step):
    t, j = STEPS[step]
    return max(0, P * (j - SUB * t))


def spread():
    out, n = [], 0
    for s in range(NSTEP):
        for place in range(PLACES):
            reached = s + (1.0 if place == PLACES - 1 else 0.15 * (place + 1))
            here = []
            while n < len(ITEMS) and ITEMS[n][0] <= reached / NSTEP:
                here.append(ITEMS[n][1])
                n += 1
            out.append(here)
    out[-1] += [i for _, i in ITEMS[n:]]
    return out


PLAN = spread()
for _t in range(SPANS - 1):
    PLAN[PLACES * (STEPS.index((_t, SUB * (_t + 1) - 1)) + 1) + 4].append(("turn", 0, _t))
PLAN[-1].append(("turn", 0, SPANS - 1))
SEGMENT = [i for place in PLAN for i in place]
FIRST_ITEMS = project(1, 0) + project(1, 1) + [i for i in SEGMENT if i[1] > 0]


DIAGONAL = [i for i in SEGMENT if i[0] == "max" and i[4] == i[2] // SUB]
RING = 3


def reader(item):
    if item[0] in ("max", "turn") or (item[0] == "trans" and item[2] < SUB and item[2] % 2):
        return "vector"
    return "scalar"


def readers(items):
    used = [reader(i) for i in items if i[0] != "rope"]
    return {engine: used.count(engine) for engine in ("vector", "scalar")}


class Segment:

    def __init__(self, a, it, half):
        self.a, self.it, self.half = a, it, half
        self.first = isinstance(a, int) and a < 0
        if self.first:
            self.places = [FIRST_ITEMS]
            self.base = {"vector": 0, "scalar": 0}
        else:
            top = UNITS - 1 - a if isinstance(a, int) else 2
            self.places = [[i for i in place if i[1] <= top] for place in PLAN]
            start, each = readers(FIRST_ITEMS), readers(SEGMENT)
            self.base = {e: start[e] + each[e] * a for e in each}
            if isinstance(a, int) and a == UNITS - 1:
                missing = readers([i for i in SEGMENT if i[1] > 1])
                self.base = {e: self.base[e] - missing[e] for e in missing}
        self.bank, self.prior, self.number = {}, {}, {}
        last, count = {}, {"vector": 0, "scalar": 0}
        for i in (i for place in self.places for i in place):
            if i[0] == "rope":
                continue
            bank = RING - 1 if i == ("turn", 0, SPANS - 1) else len(self.bank) % RING
            self.bank[i], self.prior[i] = bank, last.get(bank)
            last[bank] = i
            self.number[i] = count[reader(i)]
            count[reader(i)] += 1
        self.end = {e: self.base[e] + count[e] for e in count}

    def before(self, item):
        return self.base[reader(item)] + self.number[item]

    def unit(self, d):
        return self.a + d

    def parity(self, d):
        return (self.half + d) % 2

    def pair(self, d):
        return self.it + (self.half + d) // 2


def layer_kernel(nc, x, w_qkv, w_proj, b_proj, theta, phi, theta_noise, phi_noise, cosines, sines,
                 identity, corner, normed, heads_out, out):
    x_v = x.rearrange("b (s j p) d -> (b s) p j d", p=P, j=SUB)
    out_v = out.rearrange("b (s j p) d -> (b s) p j d", p=P, j=SUB)
    heads_v = heads_out.rearrange("(n j p) d -> n p j d", p=P, j=SUB)

    with ExitStack() as ctx:
        def sb(name, shape, dt=F32):
            return ctx.enter_context(nc.sbuf_tensor(name, shape, dt))

        def sem(name):
            return ctx.enter_context(nc.semaphore(name))

        ident = sb("ident", [P, P])
        ident_bf = sb("ident_bf", [P, P], BF16)
        diag_mask = sb("diag_mask", [P, SPAN])
        cos_t = sb("cos_t", [P, SPANS, 2 * SUB * GF])
        sin_t = sb("sin_t", [P, SPANS, 2 * SUB * GF])
        wave = sb("wave", [P, KT, 2 * DIM])
        wproj = sb("wproj", [P, KT, DIM])
        bias = sb("bias", [P, DIM])

        banks = ctx.enter_context(nc.psum_tensor("banks", [P, 8, 512], F32))
        psum = [banks[:, n, :] for n in range(8)]

        s_const = sem("const_loaded")
        s_passed = sem("waits_passed")
        s_trig_in = sem("trig_loaded")
        s_setup = sem("vector_setup")
        s_pool_setup = sem("pool_setup")
        s_xin = [sem(f"x_loaded{n}") for n in range(2)]
        s_stat = sem("stats_chain")
        s_rvar = sem("inverse_variance_ready")
        s_std = sem("inverse_deviation_ready")
        s_xn = sem("normed_ready")
        s_xt = sem("normed_turned")
        s_xte = sem("turned_copied")
        s_nout = [sem(f"normed_stored{n}") for n in range(2)]

        with ExitStack() as stage:
            def sb1(name, shape, dt=F32):
                return stage.enter_context(nc.sbuf_tensor(name, shape, dt))

            trig_a = sb1("trig_a", [P, KT, 2, DIM])
            trig_b = sb1("trig_b", [P, KT, 2, DIM])
            turns = sb1("turns", [P, KT * 2 * DIM])
            xin = sb1("xin", [P, 2, SUB, DIM])
            xn = sb1("xn", [P, 2, SUB, DIM])
            xt = sb1("xt", [P, 2, KT, SPAN])
            stats = sb1("stats", [P, SUB, 6])
            mv = sb1("mv", [P, 2, SUB, 2])
            rvar = sb1("rvar", [P, 2, SUB])
            rstd = sb1("rstd", [P, 2, SUB])

            with nc.Block() as block:
                @block.sync
                def _(sp):
                    sp.dma_start(ident[:, :], identity).then_inc(s_const, 16)
                    sp.dma_start(diag_mask[:, :], corner).then_inc(s_const, 16)
                    for src, dst, half in ((theta, trig_a, 0), (phi, trig_a, 1), (theta_noise, trig_b, 0),
                                           (phi_noise, trig_b, 1)):
                        sp.dma_start(dst[:, :, half, :], src.rearrange("(k p) n -> p k n", p=P)).then_inc(s_trig_in, 16)
                    sp.dma_start(cos_t[:, :, :], cosines).then_inc(s_const, 16)
                    sp.dma_start(sin_t[:, :, :], sines).then_inc(s_const, 16)
                    sp.dma_start(wproj[:, :, :], w_proj.rearrange("(k p) n -> p k n", p=P)).then_inc(s_const, 16)
                    sp.dma_start(bias[:, :], b_proj.rearrange("(a n) -> a n", a=1).to_broadcast([P, DIM])).then_inc(s_const, 16)
                    with sp.Fori(0, BLOCKS // 2) as it:
                        for half in range(2):
                            n = it * 2 + half
                            sp.wait_ge(s_xte, n * 2 + 2)
                            sp.dma_start(normed[n // SPANS, :, :, bass.ds((n % SPANS) * SPAN, SPAN)],
                                         xt[:, half, :, :]).then_inc(s_nout[half], 16)
                    for half in range(2):
                        sp.wait_ge(s_nout[half], 16 * (BLOCKS // 2))

                @block.gpsimd
                def _(pool):
                    pool.wait_ge(s_const, 96)
                    nc.gpsimd.tensor_copy(ident_bf[:, :], ident[:, :]).then_inc(s_pool_setup, 1)
                    for half in range(2):
                        pool.dma_start(xin[:, half, :, :], x_v[half]).then_inc(s_xin[half], 16)
                    with pool.Fori(0, BLOCKS // 2 - 1) as it:
                        for half in range(2):
                            n = it * 2 + half
                            pool.wait_ge(s_xn, n + 1)
                            pool.dma_start(xin[:, half, :, :], x_v[n + 2]).then_inc(s_xin[half], 16)

                @block.vector
                def _(dve):
                    chain = [0]

                    def link(ins):
                        chain[0] += 1
                        ins.then_inc(s_setup, 1)
                        dve.wait_ge(s_setup, chain[0])

                    two_pi = 2.0 * np.pi
                    c1 = float(np.float32(6.28125))
                    c2 = float(np.float32(two_pi - c1) - np.float32(two_pi - c1) % np.float32(2.0 ** -20))
                    c3 = float(two_pi - c1 - c2)
                    magic = float(1.5 * 2 ** 23)
                    dve.wait_ge(s_trig_in, 64)
                    flat_a = trig_a[:, :, :, :].rearrange("p k s n -> p (k s n)")
                    flat_b = trig_b[:, :, :, :].rearrange("p k s n -> p (k s n)")
                    link(nc.vector.tensor_tensor(flat_a, flat_a, flat_b, ALU.add))
                    for half in range(2):
                        view = turns[:, :].rearrange("p (k s n) -> p k s n", k=KT, s=2)[:, :, half, :]
                        link(nc.vector.tensor_scalar(view, trig_a[:, :, half, :], 1.0 / two_pi,
                                                     0.25 * (1 - half), ALU.mult, ALU.add))
                    link(nc.vector.tensor_scalar(turns[:, :], turns[:, :], magic, None, ALU.add))
                    link(nc.vector.tensor_scalar(turns[:, :], turns[:, :], -magic, None, ALU.add))
                    for c in (c1, c2, c3):
                        link(nc.vector.scalar_tensor_tensor(out=flat_a, in0=turns[:, :], scalar=-c, in1=flat_a,
                                                            op0=ALU.mult, op1=ALU.add))
                    link(nc.vector.tensor_scalar(trig_a[:, :, 0, :], trig_a[:, :, 0, :], float(np.pi / 2), None, ALU.add))
                    pi = float(np.nextafter(np.float32(np.pi), np.float32(0)))
                    link(nc.vector.tensor_scalar(flat_a, flat_a, pi, -pi, ALU.min, ALU.max))

                    assert chain[0] == REDUCE_OPS

                    def norm(n, half, loaded, reused):
                        dve.wait_ge(s_xin[half], loaded)
                        for j in range(SUB):
                            nc.vector.bn_stats(stats[:, j, :], xin[:, half, j, :]).then_inc(s_stat, 1)
                        dve.wait_ge(s_stat, n * 9 + 4)
                        dve.sem_inc(s_passed, 1)
                        for j in range(SUB):
                            dve.wait_ge(s_setup, REDUCE_OPS)
                            nc.vector.bn_aggr(mv[:, half, j, :], stats[:, j, :]).then_inc(s_stat, 1)
                        dve.wait_ge(s_stat, n * 9 + 8)
                        nc.vector.tensor_scalar(rvar[:, half, :], mv[:, half, :, 1], EPS, None, ALU.add).then_inc(s_stat, 1)
                        dve.wait_ge(s_stat, n * 9 + 9)
                        nc.vector.reciprocal(rvar[:, half, :], rvar[:, half, :]).then_inc(s_rvar, 1)
                        dve.wait_ge(s_std, n + 1)
                        if reused:
                            dve.wait_ge(s_xt, n * 2 - 2)
                        for j in range(SUB):
                            last = nc.vector.tensor_scalar(xn[:, half, j, :], xin[:, half, j, :], mv[:, half, j, 0:1],
                                                           rstd[:, half, j:j + 1], ALU.subtract, ALU.mult)
                        last.then_inc(s_xn, 1)

                    norm(0, 0, 16, False)
                    norm(1, 1, 16, False)
                    with dve.Fori(1, BLOCKS // 2) as it:
                        for half in range(2):
                            norm(it * 2 + half, half, it * 16 + 16, True)

                @block.scalar
                def _(act):
                    act.wait_ge(s_setup, REDUCE_OPS)
                    for k in range(KT):
                        nc.scalar.activation(wave[:, k, :], trig_a[:, k, :, :].rearrange("p s n -> p (s n)"),
                                             ACT.Sin)

                    def copy_out(n, half, it):
                        for k in range(KT):
                            act.wait_ge(s_xt, n * 2 + k + 1)
                            if k == 0 and it is not None:
                                act.wait_ge(s_nout[half], it * 16)
                            nc.scalar.activation(xt[:, half, k, :], psum[2 * half + k][:, :], ACT.Copy).then_inc(s_xte, 1)

                    def root(n, half):
                        act.wait_ge(s_rvar, n + 1)
                        nc.scalar.activation(rstd[:, half, :], rvar[:, half, :], ACT.Sqrt).then_inc(s_std, 1)

                    root(0, 0)
                    root(1, 1)
                    copy_out(0, 0, None)
                    root(2, 0)
                    copy_out(1, 1, None)
                    root(3, 1)
                    with act.Fori(1, BLOCKS // 2 - 1) as it:
                        for half in range(2):
                            copy_out(it * 2 + half, half, it)
                            root(it * 2 + half + 2, half)
                    for half in range(2):
                        copy_out(BLOCKS - 2 + half, half, BLOCKS // 2 - 1)

                @block.tensor
                def _(pe):
                    pe.wait_ge(s_const, 96)
                    def turn(n, half, waits):
                        pe.wait_ge(s_xn, n + 1)
                        if waits:
                            pe.wait_ge(s_xte, n * 2 - 2)
                        for k in range(KT):
                            for j in range(SUB):
                                mm = nc.tensor.transpose(psum[2 * half + k][:, j * P:(j + 1) * P],
                                                         xn[:, half, j, k * P:(k + 1) * P], ident[:, :])
                            mm.then_inc(s_xt, 1)
                    turn(0, 0, False)
                    turn(1, 1, False)
                    with pe.Fori(1, BLOCKS // 2) as it:
                        for half in range(2):
                            turn(it * 2 + half, half, True)

        with ExitStack() as stage:
            def sb2(name, shape, dt=F32):
                return stage.enter_context(nc.sbuf_tensor(name, shape, dt))

            def sem2(name):
                return stage.enter_context(nc.semaphore(name))

            xg = sb2("xg", [P, 2, KT, SPAN])
            wg = sb2("wg", [P, 2, KT, 3 * GF])
            raw = sb2("raw", [P, 2, 3, SUB, GF])
            rotated = sb2("rotated", [P, 2 * SUB * GF])
            crossed = sb2("crossed", [P, 2 * SUB * GF])
            rest = sb2("rest", [P, 2, SUB * HG, HD])
            parts = sb2("parts", [P, 2, 2, SUB * HG, SPLIT_ROWS], BF16)
            stack = [sb2(f"stack{n}", [P, 2, HG, SEQ], BF16) for n in range(2)]
            v_one = [sb2(f"v_one{n}", [P, TILES, HG, VW]) for n in range(2)]
            probs = sb2("probs", [P, 2, HG, SPAN])
            zeros = sb2("zeros", [P, HD])
            chunk_max = sb2("chunk_max", [P, SUB * HG, SPANS])
            row_max = sb2("row_max", [P, SUB, HG])
            max_rest = sb2("max_rest", [P, SUB, HG])
            max_parts = sb2("max_parts", [P, SUB, HG, MAX_ROWS], BF16)
            masked = sb2("masked", [P, 4, SPAN], BF16)
            o_raw = sb2("o_raw", [P, SPAN])
            inverse = sb2("inverse", [P, SUB * HG])
            o_norm = sb2("o_norm", [P, 2, SUB, GF])

            scores_bank = psum[0:4]
            scores_pair = [banks[:, 0:2, :], banks[:, 2:4, :]]
            ring = psum[4:4 + RING]
            out_bank = psum[7]

            s_xg = [sem2(f"span_input_loaded{n}") for n in range(2)]
            s_wg = [sem2(f"unit_weights_loaded{n}") for n in range(2)]
            s_vset = sem2("v_ones_set")
            s_vcopy = sem2("v_copied")
            s_scores = sem2("scores_ready")
            s_exp = sem2("exp_done")
            s_masked = sem2("diagonal_masked")
            s_av = sem2("values_summed")
            s_ocopy = sem2("output_copied")
            s_inv = sem2("denominators_inverted")
            s_ostore = [sem2(f"output_stored{n}") for n in range(2)]
            s_filled = {e: sem2(f"bank_filled_for_{e}") for e in ("vector", "scalar")}
            s_emptied = {e: sem2(f"bank_emptied_by_{e}") for e in ("vector", "scalar")}
            s_rope = sem2("rope_chain")
            s_msplit = sem2("maximum_split")

            N_EXP = 2 * NSTEP
            N_MSPLIT = 5 * SPANS
            N_ROPE = ROPE_OPS * SPANS

            def segments(engine, run):
                run(Segment(-1, -1, 1))
                with engine.Fori(0, UNITS // 2 - 1) as it:
                    for half in range(2):
                        run(Segment(it * 2 + half, it, half))
                for half in range(2):
                    run(Segment(UNITS - 2 + half, UNITS // 2 - 1, half))

            def filled(engine, seg, item):
                engine.wait_ge(s_filled[reader(item)], seg.before(item) + 1)

            def emptied(engine, seg, item):
                engine.wait_ge(s_emptied[reader(item)], seg.before(item) + 1)

            def to_stack(qk, bank_bf, tile):
                return (qk[0:SPLIT_ROWS, :, :, tile * P:(tile + 1) * P].rearrange("p s h n -> p (s h) n"),
                        bank_bf[0:SPLIT_ROWS, :].rearrange("p (a n) -> p a n", n=P))

            def positive(value):
                return not isinstance(value, int) or value > 0

            def rope(pool, seg, i):
                _, d, c, n = i
                done = seg.unit(d) * N_ROPE + ROPE_OPS * c + n
                if positive(done):
                    pool.wait_ge(s_rope, done)
                if n < 4:
                    flat = raw[:, c % 2, 0:2, :, :].rearrange("p s j n -> p (s j n)")
                    if n == 0:
                        emptied(pool, seg, ("qkv", d, c, 1))
                        ins = nc.gpsimd.tensor_tensor(rotated[:, :], flat, cos_t[:, c, :], ALU.mult)
                    elif n < 3:
                        e = n - 1
                        halves = flat.rearrange("p (a e d) -> p a e d", e=2, d=HD // 2)
                        sines_h = sin_t[:, c, :].rearrange("p (a e d) -> p a e d", e=2, d=HD // 2)
                        crossed_h = crossed[:, :].rearrange("p (a e d) -> p a e d", e=2, d=HD // 2)
                        ins = nc.gpsimd.tensor_tensor(crossed_h[:, :, e, :], halves[:, :, 1 - e, :], sines_h[:, :, e, :], ALU.mult)
                    else:
                        ins = nc.gpsimd.tensor_tensor(rotated[:, :], rotated[:, :], crossed[:, :], ALU.add)
                    ins.then_inc(s_rope, 1)
                    return
                k, s = (n - 4) // 2, n % 2
                last_use = ("trans", 1, SUB * ((c + 2) % SPANS) + SUB - 1)
                if n == 4 and (c >= 2 or d == 2):
                    filled(pool, seg, last_use)
                value = rotated[:, :].rearrange("p (s a d) -> p s a d", s=2, d=HD)[:, s, :, :]
                left = rest[:, s, :, :]
                by_slot = parts[:, c % 2, s, :, :].rearrange("p a (m d) -> p a m d", d=HD)
                first, last, step = (Q_SLOTS, K_SLOTS)[s][(0, 0, 1, 1)[k]]
                if k % 2 == 0:
                    src = (value, None, left)[k].unsqueeze(2)
                    count = len(range(first, last, step))
                    zero = zeros[:, :].unsqueeze(1).unsqueeze(1).to_broadcast([P, SUB * HG, count, HD])
                    ins = nc.gpsimd.tensor_tensor(by_slot[:, :, first:last:step, :],
                                                  src.to_broadcast([P, SUB * HG, count, HD]), zero, ALU.add)
                else:
                    dst = left if k == 1 else by_slot[:, :, (Q_SLOTS, K_SLOTS)[s][2][0], :]
                    ins = nc.gpsimd.tensor_tensor(dst, (value if k == 1 else left), by_slot[:, :, first, :], ALU.subtract)
                ins.then_inc(s_rope, 1)

            with nc.Block() as block:
                @block.sync
                def _(sp):
                    def load_weights(u, parity):
                        sp.dma_start(wg[:, parity, :, :], w_qkv[u % GROUPS]).then_inc(s_wg[parity], 16)

                    def load_span(u, c):
                        sp.dma_start(xg[:, c % 2, :, :],
                                     normed[u // GROUPS, :, :, c * SPAN:(c + 1) * SPAN]).then_inc(s_xg[c % 2], 16)

                    def run(seg):
                        for i in (i for place in seg.places for i in place):
                            if i[0] == "qkv" and i[3] == 1:
                                _, d, c, _ = i
                                later = seg.unit(d) + (c + 2) // SPANS
                                if isinstance(later, int) and later >= UNITS:
                                    continue
                                filled(sp, seg, i)
                                if c == 2:
                                    load_weights(later, seg.parity(d + 1))
                                load_span(later, (c + 2) % SPANS)
                            elif i[0] == "turn":
                                t = i[2]
                                emptied(sp, seg, i)
                                u = seg.a
                                sp.dma_start(heads_v[(u // GROUPS) * SPANS + t, :, :, bass.ds((u % GROUPS) * GF, GF)],
                                             o_norm[:, t % 2, :, :]).then_inc(s_ostore[t % 2], 16)

                    load_weights(0, 0)
                    load_span(0, 0)
                    load_span(0, 1)
                    segments(sp, run)
                    for n in range(2):
                        sp.wait_ge(s_ostore[n], 16 + 16 * (UNITS * SPANS // 2))

                @block.tensor
                def _(pe):
                    def item(seg, i):
                        if i[0] == "rope":
                            return
                        qk = stack[seg.parity(i[1])]
                        kind = i[0]
                        bank = ring[seg.bank[i]]
                        bank_bf = bank.bitcast(BF16)
                        if seg.prior[i] is not None:
                            emptied(pe, seg, seg.prior[i])
                        elif not seg.first:
                            pe.wait_ge(s_emptied["vector"], seg.base["vector"] - (seg.bank[i] < RING - 1))
                        if kind == "qkv":
                            _, d, c, pair = i
                            if pair == 0:
                                pe.wait_ge(s_xg[c % 2], (seg.unit(d) * 2 + c // 2 + 1) * 16)
                                if c == 0:
                                    pe.wait_ge(s_wg[seg.parity(d)], (seg.pair(d) + 1) * 16)
                            for j in range(2):
                                tile = 2 * pair + j
                                for k in range(KT):
                                    mm = nc.tensor.matmul(bank[:, j * 3 * GF:(j + 1) * 3 * GF],
                                                          xg[:, c % 2, k, tile * P:(tile + 1) * P], wg[:, seg.parity(d), k, :], start=(k == 0), stop=(k == KT - 1))
                            mm.then_inc(s_filled[reader(i)], 1)
                        elif kind == "trans":
                            c, j = i[2] // SUB, i[2] % SUB
                            if j == 0:
                                pe.wait_ge(s_rope, seg.unit(1) * N_ROPE + ROPE_OPS * (c + 1))
                            for s in range(2):
                                for h in range(HG):
                                    at = (s * HG + h) * P
                                    mm = nc.tensor.transpose(bank_bf[0:SPLIT_ROWS, at:at + P], parts[:, c % 2, s, j * HG + h, :], ident_bf[:, :])
                            mm.then_inc(s_filled[reader(i)], 1)
                        elif kind == "max":
                            _, _, tile, h, c = i
                            if h == 0 and c == 0 and tile % SUB == 0:
                                for n in ((2, 3) if tile == 0 else (3,)):
                                    emptied(pe, seg, ("trans", 1, tile + n))
                            wide = SPAN if c < tile // SUB else P * (tile % SUB + 1)
                            nc.tensor.matmul(bank[:, 0:wide], qk[0:SPLIT_ROWS, 0, h, tile * P:(tile + 1) * P],
                                             qk[0:SPLIT_ROWS, 1, h, c * SPAN:c * SPAN + wide],
                                             start=True, stop=True).then_inc(s_filled["vector"], 1)
                        elif kind == "maxrows":
                            _, d, t, half = i
                            if half == 0:
                                pe.wait_ge(s_msplit, seg.unit(d) * N_MSPLIT + 5 * (t + 1))
                            for h in range(HG):
                                for j in range(2):
                                    at = (h * 2 + j) * P
                                    mm = nc.tensor.transpose(bank_bf[SPLIT_ROWS:P, at:at + P],
                                                             max_parts[:, 2 * half + j, h, :], ident_bf[:, :])
                            mm.then_inc(s_filled[reader(i)], 1)
                        elif kind == "turn":
                            t = i[2]
                            pe.wait_ge(s_ocopy, seg.a * SPANS + t + 1)
                            for j in range(SUB):
                                mm = nc.tensor.transpose(bank[:, j * P:(j + 1) * P], o_raw[:, j * P:(j + 1) * P], ident[:, :])
                            mm.then_inc(s_filled[reader(i)], 1)

                    def scores(seg, s, h):
                        t, j = STEPS[s]
                        w0 = widths(s)
                        qk = stack[seg.parity(0)]
                        if s > 0 and h % 2 == 0:
                            pe.wait_ge(s_exp, seg.a * N_EXP + 2 * (s - 1) + h // 2 + 1)
                        if t == SPANS - 1 and j == 0 and h == 0:
                            emptied(pe, seg, LATE[1])
                        mm = nc.tensor.matmul(scores_bank[h][:, w0:SPAN], qk[:, 1, h, j * P:(j + 1) * P],
                                              qk[:, 0, h, t * SPAN + w0:(t + 1) * SPAN], start=True, stop=True)
                        if h % 2:
                            mm.then_inc(s_scores, 1)

                    def values(seg, s):
                        t, j = STEPS[s]
                        w0 = widths(s)
                        pe.wait_ge(s_exp, seg.a * N_EXP + 2 * s + 2)
                        if j >= SUB * t:
                            pe.wait_ge(s_masked, seg.a * DIAG + SUB * t + (j - SUB * t) + 1)
                        if j == 0 and t > 0:
                            pe.wait_ge(s_ocopy, seg.a * SPANS + t)
                        for h in range(HG):
                            mm = nc.tensor.matmul(out_bank[VW * h:VW * (h + 1), w0:SPAN], v_one[seg.parity(0)][:, j, h, :],
                                                  probs[:, s % 2, h, w0:SPAN],
                                                  start=(j == 0), stop=(j == SUB * (t + 1) - 1))
                        mm.then_inc(s_av, 1)

                    def run(seg):
                        if seg.first:
                            for i in seg.places[0]:
                                item(seg, i)
                            pe.wait_ge(s_emptied["vector"], seg.end["vector"])
                            return
                        pe.wait_ge(s_emptied["scalar"], seg.base["scalar"])
                        for h in range(HG):
                            scores(seg, 0, h)
                        for s in range(NSTEP):
                            for place in range(PLACES):
                                if place < HG and s + 1 < NSTEP:
                                    scores(seg, s + 1, place)
                                elif place == HG:
                                    values(seg, s)
                                for i in seg.places[PLACES * s + place]:
                                    item(seg, i)

                    pe.wait_ge(s_vset, 2)
                    segments(pe, run)

                @block.scalar
                def _(act):
                    def item(seg, i):
                        if i[0] == "rope" or reader(i) != "scalar":
                            return
                        kind, d = i[0], i[1]
                        qk = stack[seg.parity(d)]
                        bank = ring[seg.bank[i]]
                        bank_bf = bank.bitcast(BF16)
                        filled(act, seg, i)
                        if kind == "qkv":
                            _, _, c, pair = i
                            used = seg.unit(d) * N_ROPE + ROPE_OPS * (c - 2) + 3
                            if pair == 0 and positive(used):
                                act.wait_ge(s_rope, used)
                                act.wait_ge(s_vcopy, seg.unit(d) * SPANS + c - 1)
                            nc.scalar.activation(raw[:, c % 2, :, 2 * pair:2 * pair + 2, :],
                                                 bank[:, 0:6 * GF].rearrange("p (j s n) -> p s j n", j=2, s=3),
                                                 ACT.Copy).then_inc(s_emptied["scalar"], 1)
                        elif kind == "trans":
                            tile = i[2]
                            c = tile // SUB
                            if tile % SUB == 0:
                                nc.scalar.activation(v_one[seg.parity(d)][:, SUB * c:SUB * (c + 1), :, 0:HD].rearrange("p j h d -> p (j h) d"),
                                                     raw[:, c % 2, 2, :, :].rearrange("p j (h d) -> p (j h) d", h=HG),
                                                     ACT.Copy).then_inc(s_vcopy, 1)
                            nc.scalar.activation(*to_stack(qk, bank_bf, tile), ACT.Copy).then_inc(s_emptied["scalar"], 1)
                        else:
                            _, _, t, half = i
                            tile = SUB * t + 2 * half
                            nc.scalar.activation(qk[SPLIT_ROWS:P, 0, :, tile * P:(tile + 2) * P],
                                                 bank_bf[SPLIT_ROWS:P, :].rearrange("p (h n) -> p h n", h=HG),
                                                 ACT.Copy).then_inc(s_emptied["scalar"], 1)

                    def exps(seg, s, pair):
                        w0 = widths(s)
                        act.wait_ge(s_scores, seg.a * N_EXP + 2 * s + pair + 1)
                        if s >= 2 and pair == 0:
                            act.wait_ge(s_av, seg.a * NSTEP + s - 1)
                        src = scores_pair[pair][:, :, w0:SPAN]
                        nc.scalar.activation(probs[:, s % 2, 2 * pair:2 * pair + 2, w0:SPAN], src, ACT.Exp).then_inc(s_exp, 1)

                    def run(seg):
                        if seg.first:
                            for i in seg.places[0]:
                                item(seg, i)
                            return
                        exps(seg, 0, 0)
                        exps(seg, 0, 1)
                        for s in range(NSTEP):
                            t, j = STEPS[s]
                            for place in range(PLACES):
                                if place in (1, 3) and s + 1 < NSTEP:
                                    exps(seg, s + 1, place // 2)
                                elif place == HG and j == SUB * (t + 1) - 1:
                                    act.wait_ge(s_av, seg.a * NSTEP + s + 1)
                                    act.wait_ge(s_filled["vector"], seg.before(("turn", 0, t - 1)) + 1 if t else seg.base["vector"])
                                    nc.scalar.activation(o_raw[:, :], out_bank[:, :], ACT.Copy).then_inc(s_ocopy, 1)
                                for i in seg.places[PLACES * s + place]:
                                    item(seg, i)

                    act.wait_ge(s_vset, 2)
                    segments(act, run)

                @block.vector
                def _(dve):
                    def item(seg, i):
                        kind = i[0]
                        if kind == "max":
                            _, _, tile, h, c = i
                            filled(dve, seg, i)
                            bank = ring[seg.bank[i]]
                            row = (tile % SUB) * HG + h
                            to = chunk_max[:, row, c:c + 1]
                            if c < tile // SUB:
                                ins = nc.vector.tensor_reduce(to, bank[:, :], AX.X, ALU.max)
                            else:
                                wide = P * (tile % SUB + 1)
                                d = DIAGONAL.index(i)
                                if d >= 4:
                                    emptied(dve, seg, DIAGONAL[d - 4])
                                dve.sem_inc(s_passed, 1)
                                ins = nc.vector.tensor_tensor_reduce(
                                    out=masked[:, d % 4, 0:wide], in0=bank[:, 0:wide], in1=diag_mask[:, SPAN - wide:SPAN],
                                    scale=1.0, scalar=NEG, op0=ALU.add, op1=ALU.max, accum_out=to)
                            ins.then_inc(s_emptied["vector"], 1)
                            if tile % SUB == SUB - 1 and h == HG - 1 and c == tile // SUB:
                                maximum(seg, tile // SUB, i)
                        elif kind == "trans" and reader(i) == "vector":
                            filled(dve, seg, i)
                            nc.vector.tensor_copy(*to_stack(stack[seg.parity(1)], ring[seg.bank[i]].bitcast(BF16), i[2]))\
                                .then_inc(s_emptied["vector"], 1)
                        elif kind == "turn":
                            normalise(seg, i)

                    def maximum(seg, t, last):
                        base = seg.unit(1) * N_MSPLIT + 5 * t
                        emptied(dve, seg, last)
                        flat = row_max[:, :, :].rearrange("p j h -> p (j h)")
                        nc.vector.tensor_reduce(flat, chunk_max[:, :, 0:t + 1], AX.X, ALU.max).then_inc(s_msplit, 1)
                        dve.wait_ge(s_msplit, base + 1)
                        if t > 0 or not seg.first:
                            filled(dve, seg, ("maxrows", 1, t - 1, 1) if t else LATE[1])
                        nc.vector.tensor_scalar(max_parts[:, :, :, 0], row_max[:, :, :], -1.0, None, ALU.mult).then_inc(s_msplit, 1)
                        dve.wait_ge(s_msplit, base + 2)
                        nc.vector.scalar_tensor_tensor(out=max_rest[:, :, :], in0=row_max[:, :, :], scalar=-1.0,
                                                       in1=max_parts[:, :, :, 0], op0=ALU.mult, op1=ALU.subtract).then_inc(s_msplit, 1)
                        dve.wait_ge(s_msplit, base + 3)
                        nc.vector.tensor_copy(max_parts[:, :, :, 1], max_rest[:, :, :]).then_inc(s_msplit, 1)
                        dve.wait_ge(s_msplit, base + 4)
                        nc.vector.tensor_tensor(max_parts[:, :, :, 2], max_rest[:, :, :], max_parts[:, :, :, 1],
                                                ALU.subtract).then_inc(s_msplit, 1)

                    def normalise(seg, i):
                        t = i[2]
                        n = seg.a * SPANS + t
                        filled(dve, seg, i)
                        if t:
                            emptied(dve, seg, ("turn", 0, t - 1))
                        turned = ring[seg.bank[i]].rearrange("p (a d) -> p a d", d=VW)
                        nc.vector.reciprocal(inverse[:, :], turned[:, :, HD]).then_inc(s_inv, 1)
                        dve.wait_ge(s_inv, n + 1)
                        dve.wait_ge(s_ostore[t % 2], seg.a * 32 + 16 * (t // 2) + 16)
                        nc.vector.tensor_tensor(
                            o_norm[:, t % 2, :, :].rearrange("p j (h d) -> p (j h) d", h=HG),
                            turned[:, :, 0:HD],
                            inverse[:, :].unsqueeze(2).to_broadcast([P, SUB * HG, HD]),
                            ALU.mult).then_inc(s_emptied["vector"], 1)

                    def run(seg):
                        for place in seg.places:
                            for i in place:
                                item(seg, i)

                    nc.vector.memset(max_parts[:, :, :, :], 0.0)
                    for n in range(2):
                        nc.vector.memset(inverse[:, n:n + 1], 0.0).then_inc(s_ostore[n], 16)
                    for n in range(2):
                        nc.vector.memset(stack[n][SPLIT_ROWS:P, 1, :, :], 1.0)
                        nc.vector.memset(v_one[n][:, :, :, HD:VW], 1.0).then_inc(s_vset, 1)
                    segments(dve, run)

                @block.gpsimd
                def _(pool):
                    def item(seg, i):
                        if i[0] == "rope":
                            rope(pool, seg, i)

                    def mask(seg, s):
                        t, j = STEPS[s]
                        if j < SUB * t:
                            return
                        w0 = widths(s)
                        pool.wait_ge(s_exp, seg.a * N_EXP + 2 * s + 2)
                        pool.sem_inc(s_passed, 1)
                        square = probs[:, s % 2, :, w0:w0 + P]
                        nc.gpsimd.affine_select(out=square, in_=square, compare_op=ALU.is_ge, fill=0.0, base=0,
                                                pattern=[[0, HG], [1, P]], channel_multiplier=-1).then_inc(s_masked, 1)

                    def run(seg):
                        if not seg.first:
                            mask(seg, 0)
                        for n, place in enumerate(seg.places):
                            if not seg.first and n % PLACES == 3 and n // PLACES + 1 < NSTEP:
                                mask(seg, n // PLACES + 1)
                            for i in place:
                                item(seg, i)

                    nc.gpsimd.memset(zeros[:, :], 0.0).then_inc(s_pool_setup, 1)
                    pool.wait_ge(s_pool_setup, 2)
                    segments(pool, run)

        with ExitStack() as stage:
            def sb3(name, shape, dt=F32):
                return stage.enter_context(nc.sbuf_tensor(name, shape, dt))

            def sem3(name):
                return stage.enter_context(nc.semaphore(name))

            heads3 = sb3("heads3", [P, 2, SUB, DIM])
            x3 = sb3("x3", [P, 2, SUB, DIM])
            heads_t = sb3("heads_t", [P, SUB, KT * P])
            mid = sb3("mid", [P, 2, SUB, DIM])
            xn3 = sb3("xn3", [P, SUB, DIM])
            xn_t = sb3("xn_t", [P, SUB, KT * P])
            squares = sb3("squares", [P, SUB, 2 * DIM])
            power = sb3("power", [P, SUB, DIM])
            result = sb3("result", [P, 2, SUB, DIM])
            stats3 = sb3("stats3", [P, SUB, 6])
            mv3 = sb3("mv3", [P, SUB, 2])
            rvar3 = sb3("rvar3", [P, SUB])
            rstd3 = sb3("rstd3", [P, SUB])
            token = sb3("token", [P, 8])

            heads_banks = banks[:, 0:2, :].rearrange("p a (b n) -> p (a b) n", b=2)
            proj_banks = banks[:, 2:4, :].rearrange("p a (b n) -> p (a b) n", b=2)
            xn_banks = banks[:, 4:6, :].rearrange("p a (b n) -> p (a b) n", b=2)
            wave_banks = psum[6:8]

            s_load = [sem3(f"block_loaded{n}") for n in range(2)]
            s_bias = sem3("bias_added")
            s_ht = sem3("heads_turned")
            s_htc = sem3("heads_copied")
            s_proj = sem3("projected")
            s_mid = sem3("residual_added")
            s_st = sem3("stats3_chain")
            s_rv = sem3("inverse_variance3_ready")
            s_sd = sem3("inverse_deviation3_ready")
            s_xn3 = sem3("normed3_ready")
            s_nt = sem3("normed3_turned")
            s_ntc = sem3("normed3_copied")
            s_wave = sem3("waves_ready")
            s_sq = sem3("squares_ready")
            s_pow = sem3("power_ready")
            s_mod = sem3("modulus_ready")
            s_res = sem3("result_ready")
            s_store = [sem3(f"result_stored{n}") for n in range(2)]

            def first(n):
                return isinstance(n, int) and n == 0

            with nc.Block() as block:
                @block.sync
                def _(sp):
                    def load(n, half):
                        sp.dma_start(heads3[:, half, :, :], heads_v[n]).then_inc(s_load[half], 16)
                        sp.dma_start(x3[:, half, :, :], x_v[n]).then_inc(s_load[half], 16)

                    def store(n, half):
                        sp.wait_ge(s_res, n + 2)
                        sp.dma_start(out_v[n], result[:, half, :, :]).then_inc(s_store[half], 16)

                    load(0, 0)
                    load(1, 1)
                    with sp.Fori(0, BLOCKS // 2 - 1) as it:
                        for half in range(2):
                            n = it * 2 + half
                            sp.wait_ge(s_ht, n * 2 + 2)
                            sp.wait_ge(s_mid, n * 2 + 2)
                            load(n + 2, half)
                            store(n, half)
                    store(BLOCKS - 2, 0)
                    store(BLOCKS - 1, 1)
                    for half in range(2):
                        sp.wait_ge(s_store[half], 16 + 16 * (BLOCKS // 2))

                @block.tensor
                def _(pe):
                    def front(n, half, count):
                        pe.wait_ge(s_load[half], count * 32 + 32)
                        if not first(n):
                            pe.wait_ge(s_htc, n * 2)
                        for j in range(SUB):
                            for k in range(KT):
                                mm = nc.tensor.transpose(heads_banks[:, j, k * P:(k + 1) * P],
                                                         heads3[:, half, j, k * P:(k + 1) * P], ident[:, :])
                            if j % 2:
                                mm.then_inc(s_ht, 1)

                    def project(n):
                        if not first(n):
                            pe.wait_ge(s_mid, n * 2)
                        for j in range(SUB):
                            if j % 2 == 0:
                                pe.wait_ge(s_htc, n * 2 + j // 2 + 1)
                            for k in range(KT):
                                mm = nc.tensor.matmul(proj_banks[:, j, :], heads_t[:, j, k * P:(k + 1) * P], wproj[:, k, :],
                                                      start=(k == 0), stop=(k == KT - 1))
                            if j % 2:
                                mm.then_inc(s_proj, 1)

                    def turn(n):
                        pe.wait_ge(s_xn3, n + 1)
                        pe.wait_ge(s_ntc, n * 2 + 1)
                        for j in range(SUB):
                            for k in range(KT):
                                mm = nc.tensor.transpose(xn_banks[:, j, k * P:(k + 1) * P], xn3[:, j, k * P:(k + 1) * P],
                                                         ident[:, :])
                            if j % 2:
                                mm.then_inc(s_nt, 1)

                    def waves(n):
                        for j in range(SUB):
                            if j % 2 == 0:
                                pe.wait_ge(s_ntc, n * 2 + j // 2 + 2)
                            pe.wait_ge(s_sq, n * SUB + j + 1)
                            for k in range(KT):
                                mm = nc.tensor.matmul(wave_banks[j % 2], xn_t[:, j, k * P:(k + 1) * P], wave[:, k, :],
                                                      start=(k == 0), stop=(k == KT - 1))
                            mm.then_inc(s_wave, 1)

                    def front_only(n, half, count):
                        front(n, half, count)
                        project(n)

                    def step(n, half, count, has_next):
                        if has_next:
                            front(n + 1, 1 - half, count + half)
                        turn(n)
                        if has_next:
                            project(n + 1)
                        waves(n)

                    front_only(0, 0, 0)
                    with pe.Fori(0, BLOCKS // 2 - 1) as it:
                        for half in range(2):
                            step(it * 2 + half, half, it, True)
                    step(BLOCKS - 2, 0, BLOCKS // 2 - 1, True)
                    step(BLOCKS - 1, 1, BLOCKS // 2 - 1, False)

                @block.scalar
                def _(act):
                    def front(n):
                        for a in range(2):
                            act.wait_ge(s_ht, n * 2 + a + 1)
                            if a == 0 and not first(n):
                                act.wait_ge(s_proj, n * 2)
                            nc.scalar.activation(heads_t[:, 2 * a:2 * a + 2, :], heads_banks[:, 2 * a:2 * a + 2, :],
                                                 ACT.Copy).then_inc(s_htc, 1)

                    def root(n):
                        act.wait_ge(s_rv, n + 1)
                        nc.scalar.activation(rstd3[:, :], rvar3[:, :], ACT.Sqrt).then_inc(s_sd, 1)

                    def back(n):
                        for a in range(2):
                            act.wait_ge(s_nt, n * 2 + a + 1)
                            if a == 0:
                                act.wait_ge(s_wave, n * SUB + 1)
                            nc.scalar.activation(xn_t[:, 2 * a:2 * a + 2, :], xn_banks[:, 2 * a:2 * a + 2, :],
                                                 ACT.Copy).then_inc(s_ntc, 1)
                        for j in range(SUB):
                            if j == 0:
                                act.wait_ge(s_pow, n * 2 + 1)
                            act.wait_ge(s_wave, n * SUB + j + 2)
                            nc.scalar.activation(squares[:, j, :], wave_banks[j % 2], ACT.Square).then_inc(s_sq, 1)

                    def modulus(n, half, count):
                        act.wait_ge(s_pow, n * 2 + 3)
                        act.wait_ge(s_store[half], count * 16 + 16)
                        nc.scalar.activation(result[:, half, :, :], power[:, :, :], ACT.Sqrt).then_inc(s_mod, 1)

                    def step(n, half, count, has_next):
                        if has_next:
                            front(n + 1)
                        back(n)
                        if has_next:
                            root(n + 1)
                        modulus(n, half, count)

                    act.wait_ge(s_mod, 1)
                    front(0)
                    root(0)
                    with act.Fori(0, BLOCKS // 2 - 1) as it:
                        for half in range(2):
                            step(it * 2 + half, half, it, True)
                    step(BLOCKS - 2, 0, BLOCKS // 2 - 1, True)
                    step(BLOCKS - 1, 1, BLOCKS // 2 - 1, False)

                @block.vector
                def _(dve):
                    for a, (s, n) in enumerate(((s_ntc, 1), (s_sq, 2), (s_wave, 1), (s_pow, 1), (s_res, 1), (s_store[0], 16),
                                                (s_store[1], 16), (s_mod, 1))):
                        nc.vector.memset(token[:, a:a + 1], 0.0).then_inc(s, n)

                    def front(n, half):
                        dve.wait_ge(s_bias, n + 1)
                        if not first(n):
                            dve.wait_ge(s_res, n)
                        for a in range(2):
                            dve.wait_ge(s_proj, n * 2 + a + 1)
                            nc.vector.tensor_tensor(mid[:, half, 2 * a:2 * a + 2, :], proj_banks[:, 2 * a:2 * a + 2, :],
                                                    x3[:, half, 2 * a:2 * a + 2, :], ALU.add).then_inc(s_mid, 1)
                        for j in range(SUB):
                            if j % 2 == 0:
                                dve.wait_ge(s_mid, n * 2 + j // 2 + 1)
                            nc.vector.bn_stats(stats3[:, j, :], mid[:, half, j, :]).then_inc(s_st, 1)
                        dve.wait_ge(s_st, n * 9 + 4)
                        dve.sem_inc(s_passed, 1)
                        for j in range(SUB):
                            nc.vector.bn_aggr(mv3[:, j, :], stats3[:, j, :]).then_inc(s_st, 1)
                        dve.wait_ge(s_st, n * 9 + 8)
                        nc.vector.tensor_scalar(rvar3[:, :], mv3[:, :, 1], EPS, None, ALU.add).then_inc(s_st, 1)
                        dve.wait_ge(s_st, n * 9 + 9)
                        nc.vector.reciprocal(rvar3[:, :], rvar3[:, :]).then_inc(s_rv, 1)
                        dve.wait_ge(s_sd, n + 1)
                        if not first(n):
                            dve.wait_ge(s_nt, n * 2)
                        for j in range(SUB):
                            last = nc.vector.tensor_scalar(xn3[:, j, :], mid[:, half, j, :], mv3[:, j, 0:1],
                                                           rstd3[:, j:j + 1], ALU.subtract, ALU.mult)
                        last.then_inc(s_xn3, 1)

                    front(0, 0)
                    with dve.Fori(0, BLOCKS // 2 - 1) as it:
                        for half in range(2):
                            front(it * 2 + half + 1, 1 - half)
                    front(BLOCKS - 1, 1)

                @block.gpsimd
                def _(pool):
                    def front(n, half, count):
                        pool.wait_ge(s_load[half], count * 32 + 32)
                        nc.gpsimd.tensor_tensor(x3[:, half, :, :], x3[:, half, :, :],
                                                bias[:, :].unsqueeze(1).to_broadcast([P, SUB, DIM]), ALU.add).then_inc(s_bias, 1)

                    def back(n, half):
                        pool.wait_ge(s_mod, n + 1)
                        for a in range(2):
                            pool.wait_ge(s_sq, n * SUB + 2 * a + 4)
                            nc.gpsimd.tensor_tensor(power[:, 2 * a:2 * a + 2, :], squares[:, 2 * a:2 * a + 2, 0:DIM],
                                                    squares[:, 2 * a:2 * a + 2, DIM:2 * DIM], ALU.add).then_inc(s_pow, 1)
                        pool.wait_ge(s_mod, n + 2)
                        nc.gpsimd.tensor_tensor(result[:, half, :, :], result[:, half, :, :], mid[:, half, :, :],
                                                ALU.add).then_inc(s_res, 1)

                    pool.wait_ge(s_mod, 1)
                    front(0, 0, 0)
                    with pool.Fori(0, BLOCKS // 2 - 1) as it:
                        for half in range(2):
                            front(it * 2 + half + 1, 1 - half, it + half)
                            back(it * 2 + half, half)
                    front(BLOCKS - 1, 1, BLOCKS // 2 - 1)
                    back(BLOCKS - 2, 0)
                    back(BLOCKS - 1, 1)


def tables():
    inv = (np.float32(1.0) / np.float32(10000.0) ** (np.arange(0, HD, 2, dtype=np.float32) / np.float32(HD))).astype(np.float32)
    angle = np.arange(SEQ, dtype=np.float32)[:, None] * inv[None, :]
    cos, sin = np.cos(angle).astype(np.float32), np.sin(angle).astype(np.float32)
    cos, sin = np.concatenate([cos, cos], 1), np.concatenate([-sin, sin], 1)
    scale = np.array([HD ** -0.5, 1.0], np.float32)

    def lay(t):
        t = t.reshape(SPANS, SUB, P, 1, HD).transpose(2, 0, 1, 3, 4)
        t = np.broadcast_to(t[:, :, None], (P, SPANS, 2, SUB, HG, HD)) * scale[None, None, :, None, None, None]
        return np.ascontiguousarray(t.reshape(P, SPANS, 2 * SUB * GF).astype(np.float32))

    corner = np.zeros((P, SPAN), np.float32)
    corner[:, SPAN - P:] = np.where(np.arange(P)[None, :] > np.arange(P)[:, None], np.float32(NEG), np.float32(0))
    return lay(cos), lay(sin), np.eye(P, dtype=np.float32), corner


def kernel(L0_attn_x, L0_attn_w_qkv, L0_attn_w_proj, L0_attn_b_proj, L0_ffn_theta, L0_ffn_phi,
           L0_ffn_theta_noise, L0_ffn_phi_noise):
    import concourse.bacc as bacc
    from concourse.bass_utils import run_bass_kernel_spmd

    cosines, sines, eye, corner = tables()
    w_qkv = np.asarray(L0_attn_w_qkv).reshape(KT, P, 3, GROUPS, GF).transpose(3, 1, 0, 2, 4).reshape(GROUPS, P, KT, 3 * GF)
    arrays = {
        "x": L0_attn_x, "w_qkv": w_qkv, "w_proj": L0_attn_w_proj, "b_proj": L0_attn_b_proj,
        "theta": L0_ffn_theta, "phi": L0_ffn_phi, "theta_noise": L0_ffn_theta_noise, "phi_noise": L0_ffn_phi_noise,
        "cosines": cosines, "sines": sines, "eye": eye, "corner": corner,
    }
    arrays = {name: np.ascontiguousarray(a) for name, a in arrays.items()}
    nc = bacc.Bacc("TRN2", target_bir_lowering=False, num_devices=1)
    args = [nc.dram_tensor(name, a.shape, F32, kind="ExternalInput").ap() for name, a in arrays.items()]
    normed = nc.dram_tensor("normed", [BATCH, P, KT, SEQ], F32, kind="Internal").ap()
    heads_out = nc.dram_tensor("heads_out", [BATCH * SEQ, DIM], F32, kind="Internal").ap()
    out = nc.dram_tensor("out", [BATCH, SEQ, DIM], F32, kind="ExternalOutput").ap()
    layer_kernel(nc, *args, normed, heads_out, out)
    return run_bass_kernel_spmd(nc, [arrays], core_ids=[0]).results[0]["out"]
```

```python
from contextlib import ExitStack

import numpy as np

import concourse.bass as bass
from concourse import mybir
from concourse.alu_op_type import AluOpType as ALU

ACT = mybir.ActivationFunctionType
AX = mybir.AxisListType
F32 = mybir.dt.float32
BF16 = mybir.dt.bfloat16

P = 128
BATCH, SEQ, DIM, HEADS = 4, 2048, 256, 16
HD = DIM // HEADS
HG = 4
GROUPS = HEADS // HG
UNITS = BATCH * GROUPS
KT = DIM // P
SPAN = 512
SPANS = SEQ // SPAN
SUB = SPAN // P
TILES = SEQ // P
BLOCKS = BATCH * SPANS
GF = HG * HD
VW = 32
EPS = 1e-5

PARTS = 6
SPLIT_ROWS = PARTS * HD
Q_SLOTS = [(0, 3, 1), (3, 6, 2), (4, 5, 1)]
K_SLOTS = [(2, 5, 1), (1, 6, 4), (0, 1, 1)]
MAX_ROWS = P - SPLIT_ROWS
NEG = -1e30

ROPE_OPS = 12
REDUCE_OPS = 10


def share(item):
    return 1.0 if item[4] < item[2] // SUB else (item[2] % SUB + 1) / SUB


def vector_us(item):
    return 0.07 + 0.53 * share(item) if item[0] == "max" else 0.0


def project(d, c):
    return [("qkv", d, c, 0), ("qkv", d, c, 1)] + [("rope", d, c, n) for n in range(ROPE_OPS)]


def maxima(t):
    return [("max", 1, SUB * t + j, h, c) for j in range(SUB) for h in range(HG) for c in range(t + 1)]


AHEAD = [((1, 2), 0.01, 0.17), ((1, 3), 0.20, 0.25), ((2, 0), 0.48, 0.24), ((2, 1), 0.74, 0.24)]


def preparation():
    timed, now = [], 0.0

    def lay(items):
        nonlocal now
        for i in items:
            timed.append((now, i))
            now += 1.0 if i in head else vector_us(i)

    head = [("trans", 1, j) for j in range(SUB)]
    lay(head)
    for t in range(SPANS):
        chunks = maxima(t)
        trans = [("trans", 1, SUB * (t + 1) + j) for j in range(SUB)] if t + 1 < SPANS else []
        rows = [("maxrows", 1, t - 1, 0), ("maxrows", 1, t - 1, 1)] if t else []
        for n, i in enumerate(chunks):
            lay([i])
            if n in (4, 7) and rows:
                lay([rows.pop(0)])
            if trans and (n + 1 - len(chunks) // 4) * 5 > (SUB + 1 - len(trans)) * (len(chunks) * 3 // 4):
                lay([trans.pop(0)])
        lay(trans)
    for (d, c), start, length in AHEAD:
        items = project(d, c)
        for n, i in enumerate(items):
            at = start + (length * (n + 1) / len(items) if i[0] == "rope" else 0.02 * n)
            timed.append((now * at, i))
    timed += [(0.0, LATE[0]), (0.01 * now, LATE[1])]
    return sorted(((at / now * FULL, i) for at, i in timed), key=lambda p: p[0])


FULL = 1.005
LATE = [("maxrows", 0, SPANS - 1, 0), ("maxrows", 0, SPANS - 1, 1)]
ITEMS = preparation()
STEPS = [(t, j) for t in range(SPANS) for j in range(SUB * (t + 1))]
NSTEP = len(STEPS)
DIAG = SUB * SPANS
PLACES = 5


def widths(step):
    t, j = STEPS[step]
    return max(0, P * (j - SUB * t))


def spread():
    out, n = [], 0
    for s in range(NSTEP):
        for place in range(PLACES):
            reached = s + (1.0 if place == PLACES - 1 else 0.15 * (place + 1))
            here = []
            while n < len(ITEMS) and ITEMS[n][0] <= reached / NSTEP:
                here.append(ITEMS[n][1])
                n += 1
            out.append(here)
    out[-1] += [i for _, i in ITEMS[n:]]
    return out


PLAN = spread()
for _t in range(SPANS):
    PLAN[PLACES * (STEPS.index((_t, SUB * (_t + 1) - 1)) + 1) - 1].append(("save", 0, _t))
SEGMENT = [i for place in PLAN for i in place]


OPENING_BLOCKS = 9


def opening():
    norm = [("stats", 0, 0)]
    for n in range(BLOCKS):
        norm += [("stats", 0, n + 1)] if n + 1 < BLOCKS else []
        norm += [("apply", 0, n)]
        norm += [("store", 0, n - 1)] if n else []
    norm += [("store", 0, BLOCKS - 1), ("angles", 0)]

    def more(count):
        taken = norm[:count]
        del norm[:count]
        return taken

    items = more(12) + project(1, 0) + more(6) + project(1, 1) + more(OPENING_BLOCKS)
    items += [("trans", 1, j) for j in range(SUB)]
    rows = []
    for t, (d, c) in enumerate(((1, 2), (1, 3), (2, 0), (2, 1))):
        chunks = maxima(t)
        ahead = project(d, c)
        items.append(ahead.pop(0))
        trans = [("trans", 1, SUB * (t + 1) + j) for j in range(SUB)] if t + 1 < SPANS else []
        for n, i in enumerate(chunks):
            items.append(i)
            if n == 6:
                items += ahead
            if n in (4, 7) and rows:
                items.append(rows.pop(0))
            items += more(1)
            if trans and n >= len(chunks) - 2 * SUB and n % 2:
                items.append(trans.pop(0))
        rows = [("maxrows", 1, t, 0), ("maxrows", 1, t, 1)]
    return items + norm


FIRST_ITEMS = opening()
NO_BANK = ("rope", "save", "invert", "heads", "stats", "apply", "store", "angles")


DIAGONAL = [i for i in SEGMENT if i[0] == "max" and i[4] == i[2] // SUB]
LOADS = 16 * (2 * KT + 1)
X_BUFS = 3
RING = 3


def reader(item):
    if item[0] == "max" or (item[0] == "trans" and item[2] < SUB and item[2] % 2):
        return "vector"
    return "scalar"


def readers(items):
    used = [reader(i) for i in items if i[0] not in NO_BANK]
    return {engine: used.count(engine) for engine in ("vector", "scalar")}


def tail(items):
    seen, out = {"vector": 0, "scalar": 0}, {}
    banked = [i for i in items if i[0] not in NO_BANK]
    for n in reversed(range(len(banked))):
        out.setdefault(n % RING, (reader(banked[n]), seen[reader(banked[n])]))
        seen[reader(banked[n])] += 1
    return out


class Segment:

    def __init__(self, a, it, half):
        self.a, self.it, self.half = a, it, half
        self.first = isinstance(a, int) and a < 0
        if self.first:
            self.places = [FIRST_ITEMS]
            self.base = {"vector": 0, "scalar": 0}
        else:
            top = UNITS - 1 - a if isinstance(a, int) else 2
            self.places = [[i for i in place if i[1] <= top] for place in PLAN]
            before = SEGMENT
            start, each = readers(FIRST_ITEMS), readers(SEGMENT)
            self.base = {e: start[e] + each[e] * a for e in each}
            if isinstance(a, int) and a == UNITS - 1:
                missing = readers([i for i in SEGMENT if i[1] > 1])
                self.base = {e: self.base[e] - missing[e] for e in missing}
                before = [i for i in SEGMENT if i[1] <= 1]
                self.places[PLACES * 4 - 1].append(("invert", 0))
                self.places[-1].append(("heads", 0))
            self.tail = {bank: (e, self.base[e] - behind) for bank, (e, behind) in tail(before).items()}
        self.bank, self.prior, self.number = {}, {}, {}
        last, count = {}, {"vector": 0, "scalar": 0}
        for i in (i for place in self.places for i in place):
            if i[0] in NO_BANK:
                continue
            bank = len(self.bank) % RING
            self.bank[i], self.prior[i] = bank, last.get(bank)
            last[bank] = i
            self.number[i] = count[reader(i)]
            count[reader(i)] += 1
        self.end = {e: self.base[e] + count[e] for e in count}

    def before(self, item):
        return self.base[reader(item)] + self.number[item]

    def unit(self, d):
        return self.a + d

    def parity(self, d):
        return (self.half + d) % 2

    def pair(self, d):
        return self.it + (self.half + d) // 2


def layer_kernel(nc, x, w_qkv, w_proj, b_proj, theta, phi, theta_noise, phi_noise, cosines, sines,
                 identity, corner, normed, sums, inverses, out):
    x_v = x.rearrange("b (s j p) d -> (b s) p j d", p=P, j=SUB)
    out_v = out.rearrange("b (s j p) d -> (b s) p j d", p=P, j=SUB)
    sums_v = sums.rearrange("(n g p) s -> n g p s", g=GROUPS, p=P)
    sums_by_head = sums.rearrange("(n r v) s -> n r v s", r=HEADS, v=VW)
    denominator_rows = sums.rearrange("(b r v) s -> r b v s", b=BATCH, v=VW)[:, :, HD, :]
    inverse_rows = inverses.rearrange("(b r) s -> r b s", b=BATCH)
    inverse_v = inverses.rearrange("(n r) s -> n r s", r=HEADS)

    def invert_dma(sp, first, count, tile, loaded, inverted, stored):
        rows = HEADS * SPANS
        cuts = [(tile[a * rows:(a + 1) * rows, :, :], slice(a * SPAN // 2, (a + 1) * SPAN // 2)) for a in range(2)]
        for dst, columns in cuts:
            sp.dma_start(dst, denominator_rows[:, first:first + count, columns]).then_inc(loaded, 16)
        sp.wait_ge(inverted, 1)
        for src, columns in cuts:
            sp.dma_start(inverse_rows[:, first:first + count, columns], src).then_inc(stored, 16)

    with ExitStack() as ctx:
        def sb(name, shape, dt=F32):
            return ctx.enter_context(nc.sbuf_tensor(name, shape, dt))

        def sem(name):
            return ctx.enter_context(nc.semaphore(name))

        ident = sb("ident", [P, P])
        ident_bf = sb("ident_bf", [P, P], BF16)
        diag_mask = sb("diag_mask", [P, SPAN])
        cos_t = sb("cos_t", [P, SPANS, 2 * SUB, HD])
        sin_t = sb("sin_t", [P, SPANS, 2 * SUB, HD])
        wave = sb("wave", [P, KT, 2 * DIM])
        wproj = sb("wproj", [P, KT, DIM])
        bias = sb("bias", [P, DIM])

        banks = ctx.enter_context(nc.psum_tensor("banks", [P, 8, 512], F32))
        psum = [banks[:, n, :] for n in range(8)]

        x3 = sb("x3", [P, 2, SUB, DIM])
        heads_t = sb("heads_t", [P, 2, KT, SPAN])
        inverse3 = sb("inverse3", [P, 2, KT, SPAN])
        s_load = [sem(f"block_loaded{n}") for n in range(2)]
        s_heads = sem("heads_normalised")

        def load_finish(sp, n, half):
            for k in range(KT):
                heads = slice(k * HEADS // KT, (k + 1) * HEADS // KT)
                sp.dma_start(heads_t[:, half, k, :], sums_by_head[n, heads, 0:HD, :]).then_inc(s_load[half], 16)
                rows = inverse_v[n, heads, :].unsqueeze(1).to_broadcast([HEADS // KT, HD, SPAN])
                sp.dma_start(inverse3[:, half, k, :], rows).then_inc(s_load[half], 16)
            sp.dma_start(x3[:, half, :, :], x_v[n]).then_inc(s_load[half], 16)

        def normalise_heads(dve, half, loaded):
            dve.wait_ge(s_load[half], loaded)
            nc.vector.tensor_tensor(heads_t[:, half, :, :], heads_t[:, half, :, :], inverse3[:, half, :, :],
                                    ALU.mult).then_inc(s_heads, 1)

        s_ident = sem("identity_loaded")
        s_const = sem("const_loaded")
        s_passed = sem("waits_passed")
        s_late = sem("finish_constants_loaded")
        s_trig_in = sem("trig_loaded")
        s_setup = sem("vector_setup")
        s_pool_setup = sem("pool_setup")
        s_xin = [sem(f"x_loaded{n}") for n in range(X_BUFS)]
        s_stat = sem("stats_chain")
        s_rvar = sem("inverse_variance_ready")
        s_std = sem("inverse_deviation_ready")
        s_xn = sem("normed_ready")
        s_xt = sem("normed_turned")
        s_xte = sem("turned_copied")
        s_nout = [sem(f"normed_stored{n}") for n in range(2)]

        with ExitStack() as stage:
            def sb2(name, shape, dt=F32):
                return stage.enter_context(nc.sbuf_tensor(name, shape, dt))

            def sem2(name):
                return stage.enter_context(nc.semaphore(name))

            xg = sb2("xg", [P, 2, KT, SPAN])
            wg = sb2("wg", [P, 2, KT, 3 * GF])
            raw = sb2("raw", [P, 2, 3, SUB, GF])
            rotated = sb2("rotated", [P, 2 * SUB * GF])
            crossed = sb2("crossed", [P, 2 * SUB * GF])
            rest = sb2("rest", [P, 2, SUB * HG, HD])
            parts = sb2("parts", [P, 2, 2, SUB * HG, SPLIT_ROWS], BF16)
            stack = [sb2(f"stack{n}", [P, 2, HG, SEQ], BF16) for n in range(2)]
            v_one = [sb2(f"v_one{n}", [P, TILES, HG, VW]) for n in range(2)]
            probs = sb2("probs", [P, 2, HG, SPAN])
            zeros = sb2("zeros", [P, HD])
            chunk_max = sb2("chunk_max", [P, SUB * HG, SPANS])
            row_max = sb2("row_max", [P, SUB, HG])
            max_rest = sb2("max_rest", [P, SUB, HG])
            max_parts = sb2("max_parts", [P, SUB, HG, MAX_ROWS], BF16)
            masked = sb2("masked", [P, 4, SPAN], BF16)
            o_raw = sb2("o_raw", [P, 2, SPAN])
            denominators = sb2("denominators", [P, BATCH - 1, SPAN // 2])
            token = sb2("token2", [P, 2])

            trig_a = sb2("trig_a", [P, KT, 2, DIM])
            trig_b = sb2("trig_b", [P, KT, 2, DIM])
            stats = sb2("stats", [P, SUB, 6])
            mv = sb2("mv", [P, 2, SUB, 2])
            rvar = sb2("rvar", [P, 2, SUB])
            rstd = sb2("rstd", [P, 2, SUB])
            xin = [stack[1][:, 0, n, :].bitcast(F32).rearrange("p (j d) -> p j d", j=SUB) for n in range(X_BUFS)]
            turns = stack[1][:, 0, X_BUFS, :].bitcast(F32)
            xn = probs[:, 0, :, :].rearrange("p (a s) n -> p a (s n)", a=2).rearrange("p a (j d) -> p a j d", j=SUB)
            xt = probs[:, 1, :, :].rearrange("p (a k) n -> p a k n", a=2)

            scores_bank = psum[0:4]
            scores_pair = [banks[:, 0:2, :], banks[:, 2:4, :]]
            ring = psum[4:4 + RING]
            out_bank = psum[7]

            s_xg = [sem2(f"span_input_loaded{n}") for n in range(2)]
            s_wg = [sem2(f"unit_weights_loaded{n}") for n in range(2)]
            s_ones = sem2("ones_set")
            s_vcopy = sem2("v_copied")
            s_scores = sem2("scores_ready")
            s_exp = sem2("exp_done")
            s_masked = sem2("diagonal_masked")
            s_av = sem2("values_summed")
            s_ocopy = sem2("output_copied")
            s_den = sem2("denominators_loaded")
            s_inverse = sem2("denominators_inverted")
            s_inverse_out = sem2("inverses_stored")
            s_ostore = [sem2(f"output_stored{n}") for n in range(2)]
            s_filled = {e: sem2(f"bank_filled_for_{e}") for e in ("vector", "scalar")}
            s_emptied = {e: sem2(f"bank_emptied_by_{e}") for e in ("vector", "scalar")}
            s_rope = sem2("rope_chain")
            s_msplit = sem2("maximum_split")

            N_EXP = 2 * NSTEP
            N_MSPLIT = 5 * SPANS
            N_ROPE = ROPE_OPS * SPANS

            def load_block(engine, n):
                engine.dma_start(xin[n % X_BUFS], x_v[n]).then_inc(s_xin[n % X_BUFS], 16)

            def scratch_written(engine):
                for half in range(2):
                    engine.wait_ge(s_nout[half], 16 * (BLOCKS // 2))

            def segments(engine, run, opened=lambda: None):
                run(Segment(-1, -1, 1))
                opened()
                with engine.Fori(0, UNITS // 2 - 1) as it:
                    for half in range(2):
                        run(Segment(it * 2 + half, it, half))
                for half in range(2):
                    run(Segment(UNITS - 2 + half, UNITS // 2 - 1, half))

            def filled(engine, seg, item):
                engine.wait_ge(s_filled[reader(item)], seg.before(item) + 1)

            def emptied(engine, seg, item):
                engine.wait_ge(s_emptied[reader(item)], seg.before(item) + 1)

            def to_stack(qk, bank_bf, tile):
                return (qk[0:SPLIT_ROWS, :, :, tile * P:(tile + 1) * P].rearrange("p s h n -> p (s h) n"),
                        bank_bf[0:SPLIT_ROWS, :].rearrange("p (a n) -> p a n", n=P))

            def positive(value):
                return not isinstance(value, int) or value > 0

            def rope(pool, seg, i):
                _, d, c, n = i
                done = seg.unit(d) * N_ROPE + ROPE_OPS * c + n
                if positive(done):
                    pool.wait_ge(s_rope, done)
                if n < 4:
                    by_head = [t.rearrange("p (a h d) -> p a h d", h=HG, d=HD)
                               for t in (raw[:, c % 2, 0:2, :, :].rearrange("p s j n -> p (s j n)"), rotated[:, :], crossed[:, :])]
                    source, turned, cross = by_head
                    if n == 0:
                        emptied(pool, seg, ("qkv", d, c, 1))
                        table = cos_t[:, c, :, :].unsqueeze(2).to_broadcast([P, 2 * SUB, HG, HD])
                        ins = nc.gpsimd.tensor_tensor(turned, source, table, ALU.mult)
                    elif n < 3:
                        own, other = [slice(e * HD // 2, (e + 1) * HD // 2) for e in (n - 1, 2 - n)]
                        table = sin_t[:, c, :, own].unsqueeze(2).to_broadcast([P, 2 * SUB, HG, HD // 2])
                        ins = nc.gpsimd.tensor_tensor(cross[:, :, :, own], source[:, :, :, other], table, ALU.mult)
                    else:
                        ins = nc.gpsimd.tensor_tensor(rotated[:, :], rotated[:, :], crossed[:, :], ALU.add)
                    ins.then_inc(s_rope, 1)
                    return
                k, s = (n - 4) // 2, n % 2
                last_use = ("trans", 1, SUB * ((c + 2) % SPANS) + SUB - 1)
                if n == 4 and (c >= 2 or d == 2):
                    filled(pool, seg, last_use)
                value = rotated[:, :].rearrange("p (s a d) -> p s a d", s=2, d=HD)[:, s, :, :]
                left = rest[:, s, :, :]
                by_slot = parts[:, c % 2, s, :, :].rearrange("p a (m d) -> p a m d", d=HD)
                first, last, step = (Q_SLOTS, K_SLOTS)[s][(0, 0, 1, 1)[k]]
                if k % 2 == 0:
                    src = (value, None, left)[k].unsqueeze(2)
                    count = len(range(first, last, step))
                    zero = zeros[:, :].unsqueeze(1).unsqueeze(1).to_broadcast([P, SUB * HG, count, HD])
                    ins = nc.gpsimd.tensor_tensor(by_slot[:, :, first:last:step, :],
                                                  src.to_broadcast([P, SUB * HG, count, HD]), zero, ALU.add)
                else:
                    dst = left if k == 1 else by_slot[:, :, (Q_SLOTS, K_SLOTS)[s][2][0], :]
                    ins = nc.gpsimd.tensor_tensor(dst, (value if k == 1 else left), by_slot[:, :, first, :], ALU.subtract)
                ins.then_inc(s_rope, 1)

            with nc.Block() as block:
                @block.sync
                def _(sp):
                    def load_weights(u, parity):
                        sp.dma_start(wg[:, parity, :, :], w_qkv[u % GROUPS]).then_inc(s_wg[parity], 16)

                    def load_span(u, c):
                        sp.dma_start(xg[:, c % 2, :, :],
                                     normed[u // GROUPS, :, :, c * SPAN:(c + 1) * SPAN]).then_inc(s_xg[c % 2], 16)

                    def constant(dst, src, semaphore):
                        sp.dma_start(dst, src).then_inc(semaphore, 16)

                    def store_normed(n):
                        sp.dma_start(normed[n // SPANS, :, :, bass.ds((n % SPANS) * SPAN, SPAN)],
                                     xt[:, n % 2, :, :]).then_inc(s_nout[n % 2], 16)

                    def load_late():
                        for src, dst, half in ((theta, trig_a, 0), (phi, trig_a, 1), (theta_noise, trig_b, 0),
                                               (phi_noise, trig_b, 1)):
                            constant(dst[:, :, half, :], src.rearrange("(k p) n -> p k n", p=P), s_trig_in)
                        constant(wproj[:, :, :], w_proj.rearrange("(k p) n -> p k n", p=P), s_late)
                        constant(bias[:, :], b_proj.rearrange("(a n) -> a n", a=1).to_broadcast([P, DIM]), s_late)

                    def run(seg):
                        for i in (i for place in seg.places for i in place):
                            if i[0] == "store":
                                n = i[2]
                                sp.wait_ge(s_xte, n * 2 + 2)
                                store_normed(n)
                                c = {1: 0, 2: 1, 4: 2, 5: 3}.get(n)
                                if c is not None:
                                    sp.wait_ge(s_nout[c % 2], 16 * (c // 2 + 1))
                                    if c >= 2:
                                        filled(sp, seg, ("qkv", 1, c - 2, 1))
                                    load_span(0, c)
                                if n == SPANS - 1:
                                    load_late()
                            elif i[0] == "qkv" and i[3] == 1:
                                _, d, c, _ = i
                                if seg.first and d == 1 and c + 2 < SPANS:
                                    continue
                                later = seg.unit(d) + (c + 2) // SPANS
                                if isinstance(later, int) and later >= UNITS:
                                    continue
                                filled(sp, seg, i)
                                if c == 2:
                                    load_weights(later, seg.parity(d + 1))
                                load_span(later, (c + 2) % SPANS)
                            elif i[0] == "save":
                                t = i[2]
                                sp.wait_ge(s_ocopy, seg.a * SPANS + t + 1)
                                u = seg.a
                                sp.dma_start(sums_v[(u // GROUPS) * SPANS + t, u % GROUPS, :, :],
                                             o_raw[:, t % 2, :]).then_inc(s_ostore[t % 2], 16)
                            elif i[0] == "invert":
                                for n in range(2):
                                    sp.wait_ge(s_ostore[n], 16 + 16 * (SPANS // 2) * (UNITS - 1))
                                invert_dma(sp, 0, BATCH - 1, denominators, s_den, s_inverse, s_inverse_out)
                                sp.wait_ge(s_inverse_out, 32)
                                for n in range(2):
                                    load_finish(sp, n, n)

                    constant(ident[:, :], identity, s_ident)
                    for n in range(X_BUFS):
                        load_block(sp, n)
                    load_weights(0, 0)
                    constant(cos_t[:, :, :], cosines, s_const)
                    constant(sin_t[:, :, :], sines, s_const)
                    constant(diag_mask[:, :], corner, s_const)
                    segments(sp, run, lambda: scratch_written(sp))
                    for n in range(2):
                        sp.wait_ge(s_ostore[n], 16 + 16 * (UNITS * SPANS // 2))

                @block.tensor
                def _(pe):
                    def turn_block(n):
                        pe.wait_ge(s_xn, n + 1)
                        if n >= 2:
                            pe.wait_ge(s_xte, n * 2 - 2)
                        for k in range(KT):
                            for j in range(SUB):
                                mm = nc.tensor.transpose(psum[2 * (n % 2) + k][:, j * P:(j + 1) * P],
                                                         xn[:, n % 2, j, k * P:(k + 1) * P], ident[:, :])
                            mm.then_inc(s_xt, 1)

                    def item(seg, i):
                        if i[0] == "store":
                            turn_block(i[2])
                        if i[0] in NO_BANK:
                            return
                        qk = stack[seg.parity(i[1])]
                        kind = i[0]
                        bank = ring[seg.bank[i]]
                        bank_bf = bank.bitcast(BF16)
                        if seg.prior[i] is not None:
                            emptied(pe, seg, seg.prior[i])
                        elif not seg.first:
                            engine, count = seg.tail[seg.bank[i]]
                            pe.wait_ge(s_emptied[engine], count)
                        if kind == "qkv":
                            _, d, c, pair = i
                            if pair == 0:
                                pe.wait_ge(s_xg[c % 2], (seg.unit(d) * 2 + c // 2 + 1) * 16)
                                if c == 0:
                                    pe.wait_ge(s_wg[seg.parity(d)], (seg.pair(d) + 1) * 16)
                            for j in range(2):
                                tile = 2 * pair + j
                                for k in range(KT):
                                    mm = nc.tensor.matmul(bank[:, j * 3 * GF:(j + 1) * 3 * GF],
                                                          xg[:, c % 2, k, tile * P:(tile + 1) * P], wg[:, seg.parity(d), k, :], start=(k == 0), stop=(k == KT - 1))
                            mm.then_inc(s_filled[reader(i)], 1)
                        elif kind == "trans":
                            c, j = i[2] // SUB, i[2] % SUB
                            if j == 0:
                                pe.wait_ge(s_rope, seg.unit(1) * N_ROPE + ROPE_OPS * (c + 1))
                            for s in range(2):
                                for h in range(HG):
                                    at = (s * HG + h) * P
                                    mm = nc.tensor.transpose(bank_bf[0:SPLIT_ROWS, at:at + P], parts[:, c % 2, s, j * HG + h, :], ident_bf[:, :])
                            mm.then_inc(s_filled[reader(i)], 1)
                        elif kind == "max":
                            _, _, tile, h, c = i
                            if h == 0 and c == 0 and tile % SUB == 0:
                                for n in ((2, 3) if tile == 0 else (3,)):
                                    emptied(pe, seg, ("trans", 1, tile + n))
                            wide = SPAN if c < tile // SUB else P * (tile % SUB + 1)
                            nc.tensor.matmul(bank[:, 0:wide], qk[0:SPLIT_ROWS, 0, h, tile * P:(tile + 1) * P],
                                             qk[0:SPLIT_ROWS, 1, h, c * SPAN:c * SPAN + wide],
                                             start=True, stop=True).then_inc(s_filled["vector"], 1)
                        elif kind == "maxrows":
                            _, d, t, half = i
                            if half == 0:
                                pe.wait_ge(s_msplit, seg.unit(d) * N_MSPLIT + 5 * (t + 1))
                            for h in range(HG):
                                for j in range(2):
                                    at = (h * 2 + j) * P
                                    mm = nc.tensor.transpose(bank_bf[SPLIT_ROWS:P, at:at + P],
                                                             max_parts[:, 2 * half + j, h, :], ident_bf[:, :])
                            mm.then_inc(s_filled[reader(i)], 1)

                    def scores(seg, s, h):
                        t, j = STEPS[s]
                        w0 = widths(s)
                        qk = stack[seg.parity(0)]
                        if s > 0 and h % 2 == 0:
                            pe.wait_ge(s_exp, seg.a * N_EXP + 2 * (s - 1) + h // 2 + 1)
                        if t == SPANS - 1 and j == 0 and h == 0:
                            emptied(pe, seg, LATE[1])
                        mm = nc.tensor.matmul(scores_bank[h][:, w0:SPAN], qk[:, 1, h, j * P:(j + 1) * P],
                                              qk[:, 0, h, t * SPAN + w0:(t + 1) * SPAN], start=True, stop=True)
                        if h % 2:
                            mm.then_inc(s_scores, 1)

                    def values(seg, s):
                        t, j = STEPS[s]
                        w0 = widths(s)
                        pe.wait_ge(s_exp, seg.a * N_EXP + 2 * s + 2)
                        if j >= SUB * t:
                            pe.wait_ge(s_masked, seg.a * DIAG + SUB * t + (j - SUB * t) + 1)
                        if j == 0 and t > 0:
                            pe.wait_ge(s_ocopy, seg.a * SPANS + t)
                        for h in range(HG):
                            mm = nc.tensor.matmul(out_bank[VW * h:VW * (h + 1), w0:SPAN], v_one[seg.parity(0)][:, j, h, :],
                                                  probs[:, s % 2, h, w0:SPAN],
                                                  start=(j == 0), stop=(j == SUB * (t + 1) - 1))
                        mm.then_inc(s_av, 1)

                    def run(seg):
                        if seg.first:
                            for i in seg.places[0]:
                                item(seg, i)
                            pe.wait_ge(s_emptied["vector"], seg.end["vector"])
                            return
                        pe.wait_ge(s_emptied["scalar"], seg.base["scalar"])
                        for h in range(HG):
                            scores(seg, 0, h)
                        for s in range(NSTEP):
                            for place in range(PLACES):
                                if place < HG and s + 1 < NSTEP:
                                    scores(seg, s + 1, place)
                                elif place == HG:
                                    values(seg, s)
                                for i in seg.places[PLACES * s + place]:
                                    item(seg, i)

                    def opened():
                        pe.wait_ge(s_ones, 4)
                        pe.wait_ge(s_xte, 2 * BLOCKS)
                        pe.wait_ge(s_late, 32)

                    pe.wait_ge(s_ident, 16)
                    pe.wait_ge(s_pool_setup, 3)
                    segments(pe, run, opened)

                @block.scalar
                def _(act):
                    def root(n):
                        act.wait_ge(s_rvar, n + 1)
                        nc.scalar.activation(rstd[:, n % 2, :], rvar[:, n % 2, :], ACT.Sqrt).then_inc(s_std, 1)

                    def copy_block(n):
                        for k in range(KT):
                            act.wait_ge(s_xt, n * 2 + k + 1)
                            if k == 0 and n >= 2:
                                act.wait_ge(s_nout[n % 2], n // 2 * 16)
                            nc.scalar.activation(xt[:, n % 2, k, :], psum[2 * (n % 2) + k][:, :], ACT.Copy).then_inc(s_xte, 1)

                    def item(seg, i):
                        if i[0] == "stats":
                            root(i[2])
                        elif i[0] == "apply" and i[2] + X_BUFS < BLOCKS:
                            act.wait_ge(s_xn, i[2] + 1)
                            load_block(act, i[2] + X_BUFS)
                        elif i[0] == "store":
                            copy_block(i[2])
                        if i[0] in NO_BANK or reader(i) != "scalar":
                            return
                        kind, d = i[0], i[1]
                        qk = stack[seg.parity(d)]
                        bank = ring[seg.bank[i]]
                        bank_bf = bank.bitcast(BF16)
                        filled(act, seg, i)
                        if kind == "qkv":
                            _, _, c, pair = i
                            used = seg.unit(d) * N_ROPE + ROPE_OPS * (c - 2) + 3
                            if pair == 0 and positive(used):
                                act.wait_ge(s_rope, used)
                                act.wait_ge(s_vcopy, seg.unit(d) * SPANS + c - 1)
                            nc.scalar.activation(raw[:, c % 2, :, 2 * pair:2 * pair + 2, :],
                                                 bank[:, 0:6 * GF].rearrange("p (j s n) -> p s j n", j=2, s=3),
                                                 ACT.Copy).then_inc(s_emptied["scalar"], 1)
                        elif kind == "trans":
                            tile = i[2]
                            c = tile // SUB
                            if tile % SUB == 0:
                                nc.scalar.activation(v_one[seg.parity(d)][:, SUB * c:SUB * (c + 1), :, 0:HD].rearrange("p j h d -> p (j h) d"),
                                                     raw[:, c % 2, 2, :, :].rearrange("p j (h d) -> p (j h) d", h=HG),
                                                     ACT.Copy).then_inc(s_vcopy, 1)
                            nc.scalar.activation(*to_stack(qk, bank_bf, tile), ACT.Copy).then_inc(s_emptied["scalar"], 1)
                        else:
                            _, _, t, half = i
                            tile = SUB * t + 2 * half
                            nc.scalar.activation(qk[SPLIT_ROWS:P, 0, :, tile * P:(tile + 2) * P],
                                                 bank_bf[SPLIT_ROWS:P, :].rearrange("p (h n) -> p h n", h=HG),
                                                 ACT.Copy).then_inc(s_emptied["scalar"], 1)

                    def exps(seg, s, pair):
                        w0 = widths(s)
                        act.wait_ge(s_scores, seg.a * N_EXP + 2 * s + pair + 1)
                        if s >= 2 and pair == 0:
                            act.wait_ge(s_av, seg.a * NSTEP + s - 1)
                        src = scores_pair[pair][:, :, w0:SPAN]
                        nc.scalar.activation(probs[:, s % 2, 2 * pair:2 * pair + 2, w0:SPAN], src, ACT.Exp).then_inc(s_exp, 1)

                    def run(seg):
                        if seg.first:
                            for i in seg.places[0]:
                                item(seg, i)
                            return
                        exps(seg, 0, 0)
                        exps(seg, 0, 1)
                        for s in range(NSTEP):
                            t, j = STEPS[s]
                            for place in range(PLACES):
                                if place in (1, 3) and s + 1 < NSTEP:
                                    exps(seg, s + 1, place // 2)
                                elif place == HG and j == SUB * (t + 1) - 1:
                                    act.wait_ge(s_av, seg.a * NSTEP + s + 1)
                                    act.wait_ge(s_ostore[t % 2], seg.a * 32 + 16 * (t // 2) + 16)
                                    nc.scalar.activation(o_raw[:, t % 2, :], out_bank[:, :], ACT.Copy).then_inc(s_ocopy, 1)
                                for i in seg.places[PLACES * s + place]:
                                    item(seg, i)

                    def opened():
                        act.wait_ge(s_setup, REDUCE_OPS)
                        for k in range(KT):
                            nc.scalar.activation(wave[:, k, :], trig_a[:, k, :, :].rearrange("p s n -> p (s n)"), ACT.Sin)
                        scratch_written(act)

                    segments(act, run, opened)

                @block.vector
                def _(dve):
                    def reduce_angles():
                        chain = [0]

                        def link(ins):
                            chain[0] += 1
                            ins.then_inc(s_setup, 1)
                            dve.wait_ge(s_setup, chain[0])

                        two_pi = 2.0 * np.pi
                        c1 = float(np.float32(6.28125))
                        c2 = float(np.float32(two_pi - c1) - np.float32(two_pi - c1) % np.float32(2.0 ** -20))
                        c3 = float(two_pi - c1 - c2)
                        magic = float(1.5 * 2 ** 23)
                        dve.wait_ge(s_trig_in, 64)
                        flat_a = trig_a[:, :, :, :].rearrange("p k s n -> p (k s n)")
                        flat_b = trig_b[:, :, :, :].rearrange("p k s n -> p (k s n)")
                        link(nc.vector.tensor_tensor(flat_a, flat_a, flat_b, ALU.add))
                        for half in range(2):
                            view = turns.rearrange("p (k s n) -> p k s n", k=KT, s=2)[:, :, half, :]
                            link(nc.vector.tensor_scalar(view, trig_a[:, :, half, :], 1.0 / two_pi,
                                                         0.25 * (1 - half), ALU.mult, ALU.add))
                        link(nc.vector.tensor_scalar(turns, turns, magic, None, ALU.add))
                        link(nc.vector.tensor_scalar(turns, turns, -magic, None, ALU.add))
                        for c in (c1, c2, c3):
                            link(nc.vector.scalar_tensor_tensor(out=flat_a, in0=turns, scalar=-c, in1=flat_a,
                                                                op0=ALU.mult, op1=ALU.add))
                        link(nc.vector.tensor_scalar(trig_a[:, :, 0, :], trig_a[:, :, 0, :], float(np.pi / 2), None, ALU.add))
                        pi = float(np.nextafter(np.float32(np.pi), np.float32(0)))
                        link(nc.vector.tensor_scalar(flat_a, flat_a, pi, -pi, ALU.min, ALU.max))
                        assert chain[0] == REDUCE_OPS

                    def block_stats(n):
                        half = n % 2
                        dve.wait_ge(s_xin[n % X_BUFS], 16 * (n // X_BUFS + 1))
                        for j in range(SUB):
                            nc.vector.bn_stats(stats[:, j, :], xin[n % X_BUFS][:, j, :]).then_inc(s_stat, 1)
                        dve.wait_ge(s_stat, n * 9 + 4)
                        if n >= 2:
                            dve.wait_ge(s_xn, n - 1)
                        for j in range(SUB):
                            nc.vector.bn_aggr(mv[:, half, j, :], stats[:, j, :]).then_inc(s_stat, 1)
                        dve.wait_ge(s_stat, n * 9 + 8)
                        nc.vector.tensor_scalar(rvar[:, half, :], mv[:, half, :, 1], EPS, None, ALU.add).then_inc(s_stat, 1)
                        dve.wait_ge(s_stat, n * 9 + 9)
                        nc.vector.reciprocal(rvar[:, half, :], rvar[:, half, :]).then_inc(s_rvar, 1)

                    def normalise_block(n):
                        half = n % 2
                        dve.wait_ge(s_std, n + 1)
                        if n >= 2:
                            dve.wait_ge(s_xt, n * 2 - 2)
                        for j in range(SUB):
                            last = nc.vector.tensor_scalar(xn[:, half, j, :], xin[n % X_BUFS][:, j, :], mv[:, half, j, 0:1],
                                                           rstd[:, half, j:j + 1], ALU.subtract, ALU.mult)
                        last.then_inc(s_xn, 1)

                    def item(seg, i):
                        kind = i[0]
                        if kind == "stats":
                            block_stats(i[2])
                        elif kind == "apply":
                            normalise_block(i[2])
                        elif kind == "angles":
                            reduce_angles()
                        if kind == "max":
                            _, _, tile, h, c = i
                            filled(dve, seg, i)
                            bank = ring[seg.bank[i]]
                            row = (tile % SUB) * HG + h
                            to = chunk_max[:, row, c:c + 1]
                            if c < tile // SUB:
                                ins = nc.vector.tensor_reduce(to, bank[:, :], AX.X, ALU.max)
                            else:
                                wide = P * (tile % SUB + 1)
                                d = DIAGONAL.index(i)
                                if seg.first and d == 0:
                                    dve.wait_ge(s_const, 48)
                                    dve.wait_ge(s_pool_setup, 3)
                                if d >= 4:
                                    emptied(dve, seg, DIAGONAL[d - 4])
                                dve.sem_inc(s_passed, 1)
                                ins = nc.vector.tensor_tensor_reduce(
                                    out=masked[:, d % 4, 0:wide], in0=bank[:, 0:wide], in1=diag_mask[:, SPAN - wide:SPAN],
                                    scale=1.0, scalar=NEG, op0=ALU.add, op1=ALU.max, accum_out=to)
                            ins.then_inc(s_emptied["vector"], 1)
                            if tile % SUB == SUB - 1 and h == HG - 1 and c == tile // SUB:
                                maximum(seg, tile // SUB, i)
                        elif kind == "trans" and reader(i) == "vector":
                            filled(dve, seg, i)
                            nc.vector.tensor_copy(*to_stack(stack[seg.parity(1)], ring[seg.bank[i]].bitcast(BF16), i[2]))\
                                .then_inc(s_emptied["vector"], 1)
                        elif kind == "invert":
                            dve.wait_ge(s_den, 32)
                            nc.vector.reciprocal(denominators[:, :, :], denominators[:, :, :]).then_inc(s_inverse, 1)
                        elif kind == "heads":
                            for n in range(2):
                                normalise_heads(dve, n, LOADS)

                    def maximum(seg, t, last):
                        base = seg.unit(1) * N_MSPLIT + 5 * t
                        emptied(dve, seg, last)
                        flat = row_max[:, :, :].rearrange("p j h -> p (j h)")
                        nc.vector.tensor_reduce(flat, chunk_max[:, :, 0:t + 1], AX.X, ALU.max).then_inc(s_msplit, 1)
                        dve.wait_ge(s_msplit, base + 1)
                        if t > 0 or not seg.first:
                            filled(dve, seg, ("maxrows", 1, t - 1, 1) if t else LATE[1])
                        nc.vector.tensor_scalar(max_parts[:, :, :, 0], row_max[:, :, :], -1.0, None, ALU.mult).then_inc(s_msplit, 1)
                        dve.wait_ge(s_msplit, base + 2)
                        nc.vector.scalar_tensor_tensor(out=max_rest[:, :, :], in0=row_max[:, :, :], scalar=-1.0,
                                                       in1=max_parts[:, :, :, 0], op0=ALU.mult, op1=ALU.subtract).then_inc(s_msplit, 1)
                        dve.wait_ge(s_msplit, base + 3)
                        nc.vector.tensor_copy(max_parts[:, :, :, 1], max_rest[:, :, :]).then_inc(s_msplit, 1)
                        dve.wait_ge(s_msplit, base + 4)
                        nc.vector.tensor_tensor(max_parts[:, :, :, 2], max_rest[:, :, :], max_parts[:, :, :, 1],
                                                ALU.subtract).then_inc(s_msplit, 1)

                    def run(seg):
                        for place in seg.places:
                            for i in place:
                                item(seg, i)

                    def opened():
                        dve.wait_ge(s_xn, BLOCKS)

                    for n in range(2):
                        nc.vector.memset(token[:, n:n + 1], 0.0).then_inc(s_ostore[n], 16)
                    segments(dve, run, opened)

                @block.gpsimd
                def _(pool):
                    def item(seg, i):
                        if i[0] == "rope":
                            rope(pool, seg, i)

                    def mask(seg, s):
                        t, j = STEPS[s]
                        if j < SUB * t:
                            return
                        w0 = widths(s)
                        pool.wait_ge(s_exp, seg.a * N_EXP + 2 * s + 2)
                        pool.sem_inc(s_passed, 1)
                        square = probs[:, s % 2, :, w0:w0 + P]
                        nc.gpsimd.affine_select(out=square, in_=square, compare_op=ALU.is_ge, fill=0.0, base=0,
                                                pattern=[[0, HG], [1, P]], channel_multiplier=-1).then_inc(s_masked, 1)

                    def run(seg):
                        if not seg.first:
                            mask(seg, 0)
                        for n, place in enumerate(seg.places):
                            if not seg.first and n % PLACES == 3 and n // PLACES + 1 < NSTEP:
                                mask(seg, n // PLACES + 1)
                            for i in place:
                                item(seg, i)

                    nc.gpsimd.memset(zeros[:, :], 0.0).then_inc(s_pool_setup, 1)
                    nc.gpsimd.memset(max_parts[:, :, :, :], 0.0).then_inc(s_pool_setup, 1)
                    pool.wait_ge(s_ident, 16)
                    nc.gpsimd.tensor_copy(ident_bf[:, :], ident[:, :]).then_inc(s_pool_setup, 1)
                    for n in range(2):
                        nc.gpsimd.memset(v_one[n][:, :, :, HD:VW], 1.0).then_inc(s_ones, 1)
                        pool.wait_ge(s_ones, 2 * n + 1)
                        nc.gpsimd.memset(stack[n][SPLIT_ROWS:P, 1, :, :], 1.0).then_inc(s_ones, 1)
                        pool.wait_ge(s_ones, 2 * n + 2)
                    pool.wait_ge(s_const, 48)
                    pool.wait_ge(s_pool_setup, 3)
                    segments(pool, run)

        with ExitStack() as stage:
            def sb3(name, shape, dt=F32):
                return stage.enter_context(nc.sbuf_tensor(name, shape, dt))

            def sem3(name):
                return stage.enter_context(nc.semaphore(name))

            denominators3 = sb3("denominators3", [P, 1, SPAN // 2])
            mid = sb3("mid", [P, 2, SUB, DIM])
            xn3 = sb3("xn3", [P, SUB, DIM])
            xn_t = sb3("xn_t", [P, SUB, KT * P])
            squares = sb3("squares", [P, SUB, 2 * DIM])
            power = sb3("power", [P, SUB, DIM])
            result = sb3("result", [P, 2, SUB, DIM])
            stats3 = sb3("stats3", [P, SUB, 6])
            mv3 = sb3("mv3", [P, SUB, 2])
            rvar3 = sb3("rvar3", [P, SUB])
            rstd3 = sb3("rstd3", [P, SUB])
            token = sb3("token", [P, 8])

            proj_banks = banks[:, 2:4, :].rearrange("p a (b n) -> p (a b) n", b=2)
            xn_banks = banks[:, 4:6, :].rearrange("p a (b n) -> p (a b) n", b=2)
            wave_banks = psum[6:8]

            s_bias = sem3("bias_added")
            s_proj = sem3("projected")
            s_mid = sem3("residual_added")
            s_st = sem3("stats3_chain")
            s_rv = sem3("inverse_variance3_ready")
            s_sd = sem3("inverse_deviation3_ready")
            s_xn3 = sem3("normed3_ready")
            s_nt = sem3("normed3_turned")
            s_ntc = sem3("normed3_copied")
            s_wave = sem3("waves_ready")
            s_sq = sem3("squares_ready")
            s_pow = sem3("power_ready")
            s_mod = sem3("modulus_ready")
            s_res = sem3("result_ready")
            s_store = [sem3(f"result_stored{n}") for n in range(2)]

            s_den3 = sem3("denominators3_loaded")
            s_inverse3 = sem3("denominators3_inverted")
            s_inverse_out3 = sem3("inverses3_stored")

            def first(n):
                return isinstance(n, int) and n == 0

            with nc.Block() as block:
                @block.sync
                def _(sp):
                    def store(n, half):
                        sp.wait_ge(s_res, n + 2)
                        sp.dma_start(out_v[n], result[:, half, :, :]).then_inc(s_store[half], 16)

                    invert_dma(sp, BATCH - 1, 1, denominators3, s_den3, s_inverse3, s_inverse_out3)
                    sp.wait_ge(s_inverse_out3, 32)
                    with sp.Fori(0, BLOCKS // 2 - 1) as it:
                        for half in range(2):
                            n = it * 2 + half
                            sp.wait_ge(s_proj, n * 2 + 2)
                            sp.wait_ge(s_mid, n * 2 + 2)
                            load_finish(sp, n + 2, half)
                            store(n, half)
                    store(BLOCKS - 2, 0)
                    store(BLOCKS - 1, 1)
                    for half in range(2):
                        sp.wait_ge(s_store[half], 16 + 16 * (BLOCKS // 2))

                @block.tensor
                def _(pe):
                    def project(n, half):
                        pe.wait_ge(s_heads, n + 1)
                        if not first(n):
                            pe.wait_ge(s_mid, n * 2)
                        for j in range(SUB):
                            for k in range(KT):
                                mm = nc.tensor.matmul(proj_banks[:, j, :], heads_t[:, half, k, j * P:(j + 1) * P], wproj[:, k, :],
                                                      start=(k == 0), stop=(k == KT - 1))
                            if j % 2:
                                mm.then_inc(s_proj, 1)

                    def turn(n):
                        pe.wait_ge(s_xn3, n + 1)
                        pe.wait_ge(s_ntc, n * 2 + 1)
                        for j in range(SUB):
                            for k in range(KT):
                                mm = nc.tensor.transpose(xn_banks[:, j, k * P:(k + 1) * P], xn3[:, j, k * P:(k + 1) * P],
                                                         ident[:, :])
                            if j % 2:
                                mm.then_inc(s_nt, 1)

                    def waves(n):
                        for j in range(SUB):
                            if j % 2 == 0:
                                pe.wait_ge(s_ntc, n * 2 + j // 2 + 2)
                            pe.wait_ge(s_sq, n * SUB + j + 1)
                            for k in range(KT):
                                mm = nc.tensor.matmul(wave_banks[j % 2], xn_t[:, j, k * P:(k + 1) * P], wave[:, k, :],
                                                      start=(k == 0), stop=(k == KT - 1))
                            mm.then_inc(s_wave, 1)

                    def step(n, half, has_next):
                        turn(n)
                        if has_next:
                            project(n + 1, 1 - half)
                        waves(n)

                    project(0, 0)
                    with pe.Fori(0, BLOCKS // 2 - 1) as it:
                        for half in range(2):
                            step(it * 2 + half, half, True)
                    step(BLOCKS - 2, 0, True)
                    step(BLOCKS - 1, 1, False)

                @block.scalar
                def _(act):
                    def root(n):
                        act.wait_ge(s_rv, n + 1)
                        nc.scalar.activation(rstd3[:, :], rvar3[:, :], ACT.Sqrt).then_inc(s_sd, 1)

                    def back(n, has_next):
                        for a in range(2):
                            act.wait_ge(s_nt, n * 2 + a + 1)
                            if a == 0:
                                act.wait_ge(s_wave, n * SUB + 1)
                            nc.scalar.activation(xn_t[:, 2 * a:2 * a + 2, :], xn_banks[:, 2 * a:2 * a + 2, :],
                                                 ACT.Copy).then_inc(s_ntc, 1)
                        for j in range(SUB):
                            if j == 0:
                                act.wait_ge(s_pow, n * 2 + 1)
                            act.wait_ge(s_wave, n * SUB + j + 2)
                            nc.scalar.activation(squares[:, j, :], wave_banks[j % 2], ACT.Square).then_inc(s_sq, 1)
                            if j == 1 and has_next:
                                root(n + 1)

                    def modulus(n, half, count):
                        act.wait_ge(s_pow, n * 2 + 3)
                        act.wait_ge(s_store[half], count * 16 + 16)
                        nc.scalar.activation(result[:, half, :, :], power[:, :, :], ACT.Sqrt).then_inc(s_mod, 1)

                    def step(n, half, count, has_next):
                        back(n, has_next)
                        modulus(n, half, count)

                    act.wait_ge(s_mod, 1)
                    root(0)
                    with act.Fori(0, BLOCKS // 2 - 1) as it:
                        for half in range(2):
                            step(it * 2 + half, half, it, True)
                    step(BLOCKS - 2, 0, BLOCKS // 2 - 1, True)
                    step(BLOCKS - 1, 1, BLOCKS // 2 - 1, False)

                @block.vector
                def _(dve):
                    for a, (s, n) in enumerate(((s_ntc, 1), (s_sq, 2), (s_wave, 1), (s_pow, 1), (s_res, 1), (s_store[0], 16),
                                                (s_store[1], 16), (s_mod, 1))):
                        nc.vector.memset(token[:, a:a + 1], 0.0).then_inc(s, n)

                    def front(n, half):
                        dve.wait_ge(s_bias, n + 1)
                        if not first(n):
                            dve.wait_ge(s_res, n)
                        for a in range(2):
                            dve.wait_ge(s_proj, n * 2 + a + 1)
                            nc.vector.tensor_tensor(mid[:, half, 2 * a:2 * a + 2, :], proj_banks[:, 2 * a:2 * a + 2, :],
                                                    x3[:, half, 2 * a:2 * a + 2, :], ALU.add).then_inc(s_mid, 1)
                        for j in range(SUB):
                            if j % 2 == 0:
                                dve.wait_ge(s_mid, n * 2 + j // 2 + 1)
                            nc.vector.bn_stats(stats3[:, j, :], mid[:, half, j, :]).then_inc(s_st, 1)
                        dve.wait_ge(s_st, n * 9 + 4)
                        dve.sem_inc(s_passed, 1)
                        for j in range(SUB):
                            nc.vector.bn_aggr(mv3[:, j, :], stats3[:, j, :]).then_inc(s_st, 1)
                        dve.wait_ge(s_st, n * 9 + 8)
                        nc.vector.tensor_scalar(rvar3[:, :], mv3[:, :, 1], EPS, None, ALU.add).then_inc(s_st, 1)
                        dve.wait_ge(s_st, n * 9 + 9)
                        nc.vector.reciprocal(rvar3[:, :], rvar3[:, :]).then_inc(s_rv, 1)
                        dve.wait_ge(s_sd, n + 1)
                        if not first(n):
                            dve.wait_ge(s_nt, n * 2)
                        for j in range(SUB):
                            last = nc.vector.tensor_scalar(xn3[:, j, :], mid[:, half, j, :], mv3[:, j, 0:1],
                                                           rstd3[:, j:j + 1], ALU.subtract, ALU.mult)
                        last.then_inc(s_xn3, 1)

                    dve.wait_ge(s_den3, 32)
                    nc.vector.reciprocal(denominators3[:, :, :], denominators3[:, :, :]).then_inc(s_inverse3, 1)
                    front(0, 0)
                    with dve.Fori(0, BLOCKS // 2 - 1) as it:
                        for half in range(2):
                            front(it * 2 + half + 1, 1 - half)
                            normalise_heads(dve, half, it * LOADS + 2 * LOADS)
                    front(BLOCKS - 1, 1)

                @block.gpsimd
                def _(pool):
                    def front(n, half, count):
                        pool.wait_ge(s_load[half], count * LOADS + LOADS)
                        nc.gpsimd.tensor_tensor(x3[:, half, :, :], x3[:, half, :, :],
                                                bias[:, :].unsqueeze(1).to_broadcast([P, SUB, DIM]), ALU.add).then_inc(s_bias, 1)

                    def back(n, half):
                        pool.wait_ge(s_mod, n + 1)
                        for a in range(2):
                            pool.wait_ge(s_sq, n * SUB + 2 * a + 4)
                            nc.gpsimd.tensor_tensor(power[:, 2 * a:2 * a + 2, :], squares[:, 2 * a:2 * a + 2, 0:DIM],
                                                    squares[:, 2 * a:2 * a + 2, DIM:2 * DIM], ALU.add).then_inc(s_pow, 1)
                        pool.wait_ge(s_mod, n + 2)
                        nc.gpsimd.tensor_tensor(result[:, half, :, :], result[:, half, :, :], mid[:, half, :, :],
                                                ALU.add).then_inc(s_res, 1)

                    pool.wait_ge(s_mod, 1)
                    front(0, 0, 0)
                    with pool.Fori(0, BLOCKS // 2 - 1) as it:
                        for half in range(2):
                            front(it * 2 + half + 1, 1 - half, it + half)
                            back(it * 2 + half, half)
                    front(BLOCKS - 1, 1, BLOCKS // 2 - 1)
                    back(BLOCKS - 2, 0)
                    back(BLOCKS - 1, 1)


def tables():
    inv = (np.float32(1.0) / np.float32(10000.0) ** (np.arange(0, HD, 2, dtype=np.float32) / np.float32(HD))).astype(np.float32)
    angle = np.arange(SEQ, dtype=np.float32)[:, None] * inv[None, :]
    cos, sin = np.cos(angle).astype(np.float32), np.sin(angle).astype(np.float32)
    cos, sin = np.concatenate([cos, cos], 1), np.concatenate([-sin, sin], 1)
    scale = np.array([HD ** -0.5, 1.0], np.float32)

    def lay(t):
        t = t.reshape(SPANS, SUB, P, HD).transpose(2, 0, 1, 3)[:, :, None] * scale[None, None, :, None, None]
        return np.ascontiguousarray(t.reshape(P, SPANS, 2 * SUB, HD).astype(np.float32))

    corner = np.zeros((P, SPAN), np.float32)
    corner[:, SPAN - P:] = np.where(np.arange(P)[None, :] > np.arange(P)[:, None], np.float32(NEG), np.float32(0))
    return lay(cos), lay(sin), np.eye(P, dtype=np.float32), corner


def kernel(L0_attn_x, L0_attn_w_qkv, L0_attn_w_proj, L0_attn_b_proj, L0_ffn_theta, L0_ffn_phi,
           L0_ffn_theta_noise, L0_ffn_phi_noise):
    import concourse.bacc as bacc
    from concourse.bass_utils import run_bass_kernel_spmd

    cosines, sines, eye, corner = tables()
    w_qkv = np.asarray(L0_attn_w_qkv).reshape(KT, P, 3, GROUPS, GF).transpose(3, 1, 0, 2, 4).reshape(GROUPS, P, KT, 3 * GF)
    arrays = {
        "x": L0_attn_x, "w_qkv": w_qkv, "w_proj": L0_attn_w_proj, "b_proj": L0_attn_b_proj,
        "theta": L0_ffn_theta, "phi": L0_ffn_phi, "theta_noise": L0_ffn_theta_noise, "phi_noise": L0_ffn_phi_noise,
        "cosines": cosines, "sines": sines, "eye": eye, "corner": corner,
    }
    arrays = {name: np.ascontiguousarray(a) for name, a in arrays.items()}
    nc = bacc.Bacc("TRN2", target_bir_lowering=False, num_devices=1)
    args = [nc.dram_tensor(name, a.shape, F32, kind="ExternalInput").ap() for name, a in arrays.items()]
    normed = nc.dram_tensor("normed", [BATCH, P, KT, SEQ], F32, kind="Internal").ap()
    sums = nc.dram_tensor("sums", [BLOCKS * HEADS * VW, SPAN], F32, kind="Internal").ap()
    inverses = nc.dram_tensor("inverses", [BLOCKS * HEADS, SPAN], F32, kind="Internal").ap()
    out = nc.dram_tensor("out", [BATCH, SEQ, DIM], F32, kind="ExternalOutput").ap()
    layer_kernel(nc, *args, normed, sums, inverses, out)
    return run_bass_kernel_spmd(nc, [arrays], core_ids=[0]).results[0]["out"]
```
